# Optimizing a Trainium2 kernel written in Bass

```python
import numpy as np
import jax
import jax.numpy as jnp

def _softmax(x, axis=-1):
    return jax.nn.softmax(x, axis=axis)

def _gelu(x):
    return jax.nn.gelu(x, approximate=True)

def _silu(x):
    return jax.nn.silu(x)

def _sigmoid(x):
    return jax.nn.sigmoid(x)

def _layernorm(x, axis=-1, eps=1e-05):
    m = jnp.mean(x, axis=axis, keepdims=True)
    v = jnp.var(x, axis=axis, keepdims=True)
    return (x - m) / jnp.sqrt(v + eps)

def _scatter_add(tgt, idx, src, axis=0):
    return tgt.at[idx].add(src)

def _segment_sum(src, seg, n):
    return jax.ops.segment_sum(src, seg, n)
kernel_name = 'mk_adj_resnorm_d2_adj_r2_677684'

def setup_inputs(seed: int=0):
    np.random.seed(seed)
    _w = jnp.asarray

    def _rec_inputs():
        import jax
        import jax.numpy as jnp
        _gk = jax.random.key(seed)
        x = -0.000929 + 1 * jax.random.normal(jax.random.fold_in(_gk, 1), (4096, 128), jnp.float32)
        _w = (1.0 + jnp.arange(4096, dtype=jnp.float32)) ** (-0.5)
        _w = _w / _w.mean()
        _pij = jnp.clip(0.00390625 * _w[:, None] * _w[None, :], 0.0, 1.0)
        _a = jax.random.uniform(jax.random.fold_in(_gk, 2), (4096, 4096)) < _pij
        _af = _a.astype(jnp.float32)
        _af = _af * jax.random.uniform(jax.random.fold_in(_gk, 3), (4096, 4096), jnp.float32, 0.05, 0.00399995)
        adj = _af
        return (x, adj)
    x, adj = _rec_inputs()

    def _L0_gnn_setup():
        import jax, jax.numpy as jnp
        import numpy as np
        N, NFEAT, NHID, NOUT = (4096, 128, 128, 128)
        EDGE_PROB = 0.004

        def _gcn_norm_dense(adj):
            n = adj.shape[0]
            A = adj + jnp.eye(n, dtype=adj.dtype)
            deg = A.sum(axis=1)
            d = jnp.where(deg > 0, jax.lax.rsqrt(deg), 0.0)
            return d[:, None] * A * d[None, :]
        key = jax.random.key(seed)
        k_x, k_a, k_w1, k_w2 = jax.random.split(key, 4)
        x = jax.random.normal(k_x, (N, NFEAT), dtype=jnp.float32)
        a = jax.random.uniform(k_a, (N, N), dtype=jnp.float32)
        adj = jnp.where(a < EDGE_PROB, a, 0.0)
        adj = adj.at[jnp.diag_indices(N)].set(0.0)
        W1 = jax.random.normal(k_w1, (NFEAT, NHID), dtype=jnp.float32) * (1.0 / np.sqrt(NFEAT))
        b1 = jnp.zeros((NHID,), dtype=jnp.float32)
        W2 = jax.random.normal(k_w2, (NHID, NOUT), dtype=jnp.float32) * (1.0 / np.sqrt(NHID))
        b2 = jnp.zeros((NOUT,), dtype=jnp.float32)
        return {'x': x, 'adj': adj, 'W1': W1, 'b1': b1, 'W2': W2, 'b2': b2}
    _L0_gnn_all = _L0_gnn_setup()
    _L0_gnn_in = {k: v for k, v in _L0_gnn_all.items() if k in ('W1', 'b1', 'W2', 'b2')}
    del _L0_gnn_all

    def _L1_gnn_setup():
        import jax, jax.numpy as jnp
        import numpy as np
        K = 2
        NEG = -9000000000000000.0
        N, C, CO = (3072, 128, 128)

        def _ln(x, g, b, eps=1e-05):
            m = x.mean(-1, keepdims=True)
            v = ((x - m) ** 2).mean(-1, keepdims=True)
            return (x - m) / jnp.sqrt(v + eps) * g + b
        key = jax.random.key(seed)
        ks = jax.random.split(key, 6)
        x = jax.random.normal(ks[0], (N, C), jnp.float32)
        adj = (jax.random.uniform(ks[1], (N, N)) < 0.01).astype(jnp.float32)
        ff0_w = jax.random.normal(ks[2], (K, C, C), jnp.float32) / np.float32(np.sqrt(C))
        ff1_w = jax.random.normal(ks[3], (K, CO, C), jnp.float32) / np.float32(np.sqrt(C))
        attn_w = jax.random.normal(ks[4], (K, 2 * C), jnp.float32) / np.float32(np.sqrt(2 * C))
        return dict(x=x, adj=adj, ff0_w=ff0_w, ff1_w=ff1_w, attn_w=attn_w, g1=jnp.ones((C,), jnp.float32), b1=jnp.zeros((C,), jnp.float32), g2=jnp.ones((C,), jnp.float32), b2=jnp.zeros((C,), jnp.float32))
    _L1_gnn_all = _L1_gnn_setup()
    _L1_gnn_in = {k: v for k, v in _L1_gnn_all.items() if k in ('ff0_w', 'ff1_w', 'attn_w', 'g1', 'b1', 'g2', 'b2')}
    del _L1_gnn_all
    return {'x': x, 'adj': adj, 'L0_gnn_W1': _L0_gnn_in['W1'], 'L0_gnn_b1': _L0_gnn_in['b1'], 'L0_gnn_W2': _L0_gnn_in['W2'], 'L0_gnn_b2': _L0_gnn_in['b2'], 'L1_gnn_ff0_w': _L1_gnn_in['ff0_w'], 'L1_gnn_ff1_w': _L1_gnn_in['ff1_w'], 'L1_gnn_attn_w': _L1_gnn_in['attn_w'], 'L1_gnn_g1': _L1_gnn_in['g1'], 'L1_gnn_b1': _L1_gnn_in['b1'], 'L1_gnn_g2': _L1_gnn_in['g2'], 'L1_gnn_b2': _L1_gnn_in['b2']}

def reference(x, adj, L0_gnn_W1, L0_gnn_b1, L0_gnn_W2, L0_gnn_b2, L1_gnn_ff0_w, L1_gnn_ff1_w, L1_gnn_attn_w, L1_gnn_g1, L1_gnn_b1, L1_gnn_g2, L1_gnn_b2):
    import jax
    import jax.numpy as jnp

    def _L0_gnn_ref(x, adj, W1, b1, W2, b2):
        import jax, jax.numpy as jnp
        import numpy as np
        N, NFEAT, NHID, NOUT = (4096, 128, 128, 128)
        EDGE_PROB = 0.004

        def _gcn_norm_dense(adj):
            n = adj.shape[0]
            A = adj + jnp.eye(n, dtype=adj.dtype)
            deg = A.sum(axis=1)
            d = jnp.where(deg > 0, jax.lax.rsqrt(deg), 0.0)
            return d[:, None] * A * d[None, :]
        An = _gcn_norm_dense(adj)
        h = jax.nn.relu(An @ (x @ W1) + b1)
        out = An @ (h @ W2) + b2
        return out

    def _L1_gnn_ref(x, adj, ff0_w, ff1_w, attn_w, g1, b1, g2, b2):
        import jax, jax.numpy as jnp
        import numpy as np
        K = 2
        NEG = -9000000000000000.0
        N, C, CO = (3072, 128, 128)

        def _ln(x, g, b, eps=1e-05):
            m = x.mean(-1, keepdims=True)
            v = ((x - m) ** 2).mean(-1, keepdims=True)
            return (x - m) / jnp.sqrt(v + eps) * g + b
        n, c = x.shape
        co = ff1_w.shape[1]
        x_norm = _ln(x, g1, b1)
        mask = (adj > 0) | jnp.eye(n, dtype=bool)
        h_next = jnp.zeros((n, co), x.dtype)
        for i in range(K):
            h = x_norm @ ff0_w[i].T
            s_src = h @ attn_w[i, :c]
            s_dst = h @ attn_w[i, c:]
            e = jax.nn.leaky_relu(s_src[:, None] + s_dst[None, :])
            e = jnp.where(mask, e, jnp.float32(NEG))
            atten = jax.nn.softmax(e, axis=1)
            att = atten @ h + x
            att = _ln(att, g2, b2)
            h_next = h_next + jax.nn.elu(att @ ff1_w[i].T) / K
        return h_next
    x = _layernorm(x + _L0_gnn_ref(x, adj, L0_gnn_W1, L0_gnn_b1, L0_gnn_W2, L0_gnn_b2), axis=-1)
    x = _layernorm(x + _L1_gnn_ref(x, adj, L1_gnn_ff0_w, L1_gnn_ff1_w, L1_gnn_attn_w, L1_gnn_g1, L1_gnn_b1, L1_gnn_g2, L1_gnn_b2), axis=-1)
    return x

_drawn_inputs = setup_inputs


def setup_inputs(seed=0):
    import zlib

    import numpy as np

    out = dict(_drawn_inputs(seed))
    spreads = {'L0_gnn_b1': (0.0, 0.1),
     'L0_gnn_b2': (0.0, 0.1),
     'L1_gnn_g1': (1.0, 0.2),
     'L1_gnn_b1': (0.0, 0.1),
     'L1_gnn_g2': (1.0, 0.2),
     'L1_gnn_b2': (0.0, 0.1)}
    factors = {}
    for name, (base, spread) in spreads.items():
        noise = np.random.default_rng([zlib.crc32(name.encode()), seed]).standard_normal(out[name].shape)
        drawn = base * np.exp(spread * noise) if base else spread * noise
        out[name] = jnp.asarray(drawn.astype(out[name].dtype))
    for name, factor in factors.items():
        out[name] = (out[name] * factor).astype(out[name].dtype)
    return out
```

```python
from contextlib import ExitStack

import concourse.bass as bass
from concourse import mybir

F32 = mybir.dt.float32
F32R = mybir.dt.float32r
BF16 = mybir.dt.bfloat16
U8 = mybir.dt.uint8
I32 = mybir.dt.int32
ALU = mybir.AluOpType
ACT = mybir.ActivationFunctionType
AX_X = mybir.AxisListType.X

P = 128
GW = 512
BPG = GW // P
JC = 4
RING = 4
MVW = 2 * (P + 1)
WINDOW = 64.0
LN_EPS = 1e-5
TINY = 1e-30


def bcast(column, n):
    return column.unsqueeze(2).broadcast_to([column.shape[0], column.shape[1], n])


def build(nc, t, out):
    N, C = t["x"].shape
    K = t["ff0"].shape[0]
    B = N // P
    NG = N // GW
    NC = B // JC
    NI = B // RING
    assert C == P and K == 2 and NG <= 8 and NC % 2 == 0

    mask_dram = nc.dram_tensor("mask_by_group", [NG, P, B, GW], U8).ap()

    ctx = ExitStack()
    with ctx:
        block_scope = ctx

        def sb(name, shape, dtype, scope=None):
            return (scope or block_scope).enter_context(nc.sbuf_tensor(name, shape, dtype))

        def sem(name):
            return block_scope.enter_context(nc.semaphore(name))

        x1 = sb("x1", [P, B, C], F32)
        xnT_acc = sb("xnT_acc", [P, B, C], F32)
        ident = sb("ident", [P, P], F32)
        ident2 = sb("ident2", [P, P], U8)
        zeros = sb("zeros", [P, GW], BF16)
        w1 = sb("w1", [P, C], F32)
        w2 = sb("w2", [P, C], F32)
        b1bc = sb("b1bc", [P, C], F32)
        b2bc = sb("b2bc", [P, C], F32)
        vec = sb("vec", [P, 4], F32)
        ff0 = sb("ff0", [P, K, C], F32)
        ff0T = sb("ff0T", [P, K, C], F32)
        ff1T = sb("ff1T", [P, K, C], F32)
        attnT = sb("attnT", [P, K, 2], F32)
        wa = sb("wa", [P, K * 2], F32)
        was = sb("was", [P, P], F32)
        half = sb("half", [P, B], F32)
        d_all = sb("d_all", [P, B], F32)
        d2_all = sb("d2_all", [P, B], F32)
        small = sb("small", [P, 16], F32)
        bn = sb("bn", [P, B, 6], F32)
        mv = sb("mv", [P, B, 2], F32)
        rstd = sb("rstd", [P, B], F32)
        r2 = sb("r2", [P, B], F32)
        shift = sb("shift", [P, B], F32)
        st = sb("st", [P, B, K * 2], F32)
        span = sb("span", [P, 2 * K], F32)
        top = sb("top", [P, 2 * K], F32)
        npass_f = sb("npass_f", [P, 2], F32)
        npass = sb("npass", [P, 1], I32)
        gref = sb("gref", [P, 2], F32)
        uu = sb("uu", [P, B], F32)
        vv = sb("vv", [P, B], F32)
        UU = sb("UU", [P, B], F32)
        VV = sb("VV", [P, B], F32)
        mstar = sb("mstar", [P, B], F32)
        tm = [sb(f"tm{n}", [P, B], F32) for n in range(5)]

        first = ExitStack()
        rowbuf = sb("rowbuf", [P, 2, N], F32, first)
        colbuf = sb("colbuf", [P, RING, N], F32, first)
        xw_g = sb("xw_g", [P, B, C], F32, first)
        mtile = sb("mtile", [P, 2, N], U8, first)
        stat = sb("stat", [P, RING, C], F32, first)
        diag = sb("diag", [P, RING, C], F32, first)
        hT = sb("hT", [P, 2, GW], F32, first)
        part = sb("part", [P, 8], F32, first)
        first.close()

        MV = [sb(f"MV{w}", [P, B, MVW], F32R) for w in range(2)]
        h = sb("h", [P, B, C], F32)
        negs = sb("negs", [P, N], F32)
        PQ = sb("PQ", [P, 2, 2, JC, GW], F32R)
        X = sb("X", [P, 2, JC, GW], BF16)
        mring = sb("mring", [P, 2, JC, GW], U8)
        num = sb("num", [P, B, C + 1], F32)
        ev = sb("ev", [P, 2, 2, MVW], F32)
        tbuf = X[:, :, :, :].rearrange("p a b c -> p (a b c)").bitcast(F32).rearrange("p (a n) -> p a n", a=4)

        ps = ctx.enter_context(nc.psum_tensor("ps", [P, 8, GW], F32))


        def sems(names):
            return [sem(name) for name in names.split()]

        consts, ident_ready, zeros_ready, xb2_ready = sems("consts ident_ready zeros_ready xb2_ready")
        row_loaded = sems("row_loaded0 row_loaded1")
        col_loaded = [sem(f"col_loaded{s}") for s in range(RING)]
        mask_stored = sems("mask_stored0 mask_stored1")
        mask_loaded = sems("mask_loaded0 mask_loaded1")
        xw_done, xw_ready, rowsum_done, deg_step, deg_ready, pow_ready = sems(
            "xw_done xw_ready rowsum_done deg_step deg_ready pow_ready")
        stat_ready, pe_block, agg_done, hT_ready, hw_done, g_ready, g_copied, mask_made, tile_step = sems(
            "stat_ready pe_block agg_done hT_ready hw_done g_ready g_copied mask_made tile_step")
        dve_step, accT_ready, tr_done, var_ready, rstd_ready, shift_ready, xn_ready, xnt_done, xnT_ready = sems(
            "dve_step accT_ready tr_done var_ready rstd_ready shift_ready xn_ready xnt_done xnT_ready")
        wa_done, wa_ready, st_done, st_ready, span_ready, top_ready, npass_ready, was_ready = sems(
            "wa_done wa_ready st_done st_ready span_ready top_ready npass_ready was_ready")
        h_done, h_ready, s_done, negs_ready, num_zeroed, pass_step, factors_ready, exp_ready = sems(
            "h_done h_ready s_done negs_ready num_zeroed pass_step factors_ready exp_ready")
        prod_ready, hi_ready, mv_ready, x_made, p_made, q_made, bank_done = sems(
            "prod_ready hi_ready mv_ready x_made p_made q_made bank_done")
        ev_ready, num_added, add_step, att_ready, att_t_done, att_t_ready, y_done, y_read, elu_used, out_ready, stored, loads_started = sems(
            "ev_ready num_added add_step att_ready att_t_done att_t_ready y_done y_read elu_used out_ready stored loads_started")

        last_var_ready, last_rstd_ready = sems("last_var_ready last_rstd_ready")

        adj_rows = t["adj"].rearrange("(b p) n -> b p n", p=P)
        adj_cols = t["adjT"].rearrange("(b p) n -> b p n", p=P)
        out_v = out.rearrange("(b p) c -> p b c", p=P)
        xnT = xnT_acc[:, :, :].rearrange("p b c -> p (b c)")
        acc = xnT_acc

        prod = [ev[:, w, :, :].rearrange("p a n -> p (a n)")[:, 0:GW] for w in range(2)]

        def block_of(tensor, b):
            return tensor[:, bass.ds(b, 1), :].rearrange("p o n -> p (o n)")

        def dram_block(tensor, b):
            return tensor[bass.ds(b, 1), :, :].rearrange("o p n -> (o p) n")

        def group(k):
            return slice(k * BPG, (k + 1) * BPG)

        def cols(k, n=P):
            return slice(k * n, (k + 1) * n)

        CONSTS = [
            (xnT, t["xT"]), (w1[:, :], t["W1"]), (w2[:, :], t["W2"]),
            (b1bc[:, :], t["b1"].partition_broadcast(P)), (b2bc[:, :], t["b2"].partition_broadcast(P)),
            (ff0[:, :, :], t["ff0"].rearrange("k o i -> o k i")),
            (ff0T[:, :, :], t["ff0T"].rearrange("k i o -> i k o")),
            (ff1T[:, :, :], t["ff1T"].rearrange("k i o -> i k o")),
            (attnT[:, :, :], t["attnT"]),
            (x1[:, :, :], t["x"].rearrange("(b p) c -> p b c", p=P)),
        ] + [(vec[:, m:m + 1], t[name].rearrange("(p o) -> p o", o=1))
             for m, name in enumerate(("ln1_g", "ln1_b", "ln2_g", "ln2_b"))]
        ALL_CONSTS = 16 * len(CONSTS)

        ROW_CREDIT, COL_CREDIT, X_CREDIT, PQ_CREDIT, BANK_CREDIT, EV_CREDIT = 2, RING, 2 * JC, 2, 2 * BPG, 2
        STORE_CREDIT = 16
        MASK_CREDIT = B + COL_CREDIT
        BANKS = 2 * BPG
        DONE_CREDIT = 2 * BANKS
        GC = NG * NC
        PASS_STEPS = 18
        SN = 2
        MAX_PASSES = 1 << 12

        def passes(eng):
            eng.wait_ge(npass_ready, 1)
            return eng.value_load(npass[0:1, 0:1], min_val=1, max_val=MAX_PASSES)

        block = ctx.enter_context(nc.Block())

        @block.sync
        def _(sp):
            with sp.Fori(0, NI) as i:
                for u in range(RING):
                    b = i * RING + u
                    sp.wait_ge(rowsum_done, b + 1)
                    sp.dma_start(rowbuf[:, u % 2, :], dram_block(adj_rows, b)).then_inc(row_loaded[u % 2], 16)
                    sp.wait_ge(pe_block, b + 1)
                    sp.dma_start(colbuf[:, u, :], dram_block(adj_cols, b)).then_inc(col_loaded[u], 16)
            with sp.Fori(0, NI) as i:
                for u in range(RING):
                    b = i * RING + u
                    sp.wait_ge(pe_block, b + B + 1)
                    sp.wait_ge(mask_made, b + B + 1)
                    sp.dma_start(colbuf[:, u, :], dram_block(adj_cols, b)).then_inc(col_loaded[u], 16)
            for s in range(SN):
                sp.wait_ge(mask_stored[s], 16 * (B // SN) + STORE_CREDIT)
            n = passes(sp)
            with sp.Fori(0, n * K) as q:
                with sp.Fori(0, NG) as g:
                    for c in range(NC):
                        sp.wait_ge(x_made, (q * GC + g * NC + c + 1) * JC)
                        sp.sem_inc(loads_started, 1)
                        sp.dma_start(mring[:, c % SN, :, :],
                                     mask_dram[bass.ds(g, 1), :, cols(c, JC), :].rearrange("o p b n -> (o p) b n"))\
                            .then_inc(mask_loaded[c % SN], 16)
            for k in range(NG):
                sp.wait_ge(out_ready, k + 1)
                sp.dma_start(out_v[:, group(k), :], acc[:, group(k), :]).then_inc(stored, 16)
            sp.wait_ge(stored, 16 * NG)

        @block.gpsimd
        def _(pool):
            pool.sem_inc(num_added, EV_CREDIT)
            pool.memset(ident[:, :], 0.0).then_inc(ident_ready, 1)
            pool.memset(half[:, :], -0.5).then_inc(ident_ready, 1)
            pool.wait_ge(ident_ready, 2)
            pool.affine_select(out=ident[:, :], in_=ident[:, :], compare_op=ALU.not_equal, fill=1.0, base=0,
                               pattern=[[-1, P]], channel_multiplier=1).then_inc(ident_ready, 1)
            pool.wait_ge(ident_ready, 3)
            pool.tensor_scalar(ident2[:, :], ident[:, :], 2.0, 0.0, ALU.mult, ALU.add).then_inc(ident_ready, 1)
            pool.wait_ge(consts, ALL_CONSTS)
            pool.tensor_tensor(x1[:, :, :], x1[:, :, :], b2bc[:, :].unsqueeze(1).broadcast_to([P, B, C]), ALU.add)\
                .then_inc(xb2_ready, 1)
            with pool.Fori(0, B) as b:
                pool.wait_ge(deg_ready, b + 1)
                pool.tensor_tensor(small[:, 3:4], small[:, 1:2], half[:, 0:1], ALU.pow).then_inc(pow_ready, 1)
            for k in range(NG):
                pool.wait_ge(var_ready, 2 * k + 1)
                pool.tensor_tensor(rstd[:, group(k)], rstd[:, group(k)], half[:, group(k)], ALU.pow)\
                    .then_inc(rstd_ready, 1)
                pool.wait_ge(var_ready, 2 * k + 2)
                pool.tensor_tensor(r2[:, group(k)], r2[:, group(k)], half[:, group(k)], ALU.pow).then_inc(rstd_ready, 1)
            pool.wait_ge(span_ready, 1)
            pool.partition_all_reduce(top[:, :], span[:, :], P, bass.bass_isa.ReduceOp.max).then_inc(top_ready, 1)
            n = passes(pool)
            for head in range(K):
                if head:
                    pool.wait_ge(att_t_done, head * NG)
                pool.memset(num[:, :, :], 0.0).then_inc(num_zeroed, 1)
                pool.wait_ge(num_zeroed, head + 1)
                with pool.Fori(n * head, n * (head + 1)) as q:
                    with pool.Fori(0, NG) as g:
                        for ib in range(BPG):
                            e = (q * NG + g) * BPG + ib
                            s = ev[:, ib % SN, 0, :]
                            row = block_of(num, g * BPG + ib)
                            pool.wait_ge(ev_ready, e * 2 + (2 + BANK_CREDIT))
                            pool.tensor_tensor(s, s, ev[:, ib % SN, 1, :], ALU.add).then_inc(add_step, 1)
                            pool.wait_ge(add_step, e * 2 + 1)
                            pool.tensor_tensor(s[:, 0:C + 1], s[:, 0:C + 1], s[:, C + 1:MVW], ALU.add)\
                                .then_inc(add_step, 1)
                            pool.wait_ge(add_step, e * 2 + 2)
                            pool.tensor_tensor(row, row, s[:, 0:C + 1], ALU.add).then_inc(num_added, 1)
                for k in range(NG + 1):
                    if k < NG:
                        pool.wait_ge(var_ready, (2 + head) * NG + k + 1)
                        pool.tensor_tensor(rstd[:, group(k)], rstd[:, group(k)], half[:, group(k)], ALU.pow)\
                            .then_inc(rstd_ready, 1)
                    if k and head == K - 1:
                        pool.wait_ge(last_var_ready, k)
                        pool.tensor_tensor(r2[:, group(k - 1)], r2[:, group(k - 1)], half[:, group(k - 1)], ALU.pow)\
                            .then_inc(last_rstd_ready, 1)

        @block.scalar
        def _(act):
            for dst, src in CONSTS:
                act.dma_start(dst, src).then_inc(consts, 16)
            act.sem_inc(q_made, PQ_CREDIT)
            act.sem_inc(ev_ready, BANK_CREDIT)
            for s in range(SN):
                act.sem_inc(mask_stored[s], STORE_CREDIT)
            for k in range(NG):
                act.wait_ge(xw_done, k + 1)
                act.activation(xw_g[:, group(k), :].rearrange("p b c -> p (b c)"), ps[:, k, :], ACT.Copy)\
                    .then_inc(xw_ready, 1)
            for k in range(NG):
                act.wait_ge(agg_done, k + 1)
                if k >= SN:
                    act.wait_ge(hw_done, k - 1)
                act.activation(hT[:, k % SN, :], ps[:, k, :], ACT.Relu).then_inc(hT_ready, 1)
            act.wait_ge(g_ready, NG)
            with act.Fori(0, NI) as i:
                for u in range(RING):
                    b = i * RING + u
                    act.wait_ge(pe_block, b + B + 1)
                    act.activation(stat[:, u, :], block_of(xw_g, b), ACT.Copy).then_inc(g_copied, 1)
                    act.wait_ge(mask_made, b + (1 + MASK_CREDIT))
                    act.dma_start(mask_dram[:, :, bass.ds(b, 1), :].rearrange("g p o n -> p g (o n)"),
                                  mtile[:, u % SN, :].rearrange("p (g n) -> p g n", n=GW))\
                        .then_inc(mask_stored[u % SN], 16)

            def xnT_group(k):
                act.wait_ge(shift_ready, k + 1)
                for b in range(k * BPG, (k + 1) * BPG):
                    act.activation(h[:, b, :], x1[:, b, :], ACT.Identity, scale=r2[:, b:b + 1], bias=shift[:, b:b + 1])\
                        .then_inc(xn_ready, 1)
                act.wait_ge(xnt_done, k + 1)
                act.activation(xnT[:, cols(k, GW)], ps[:, k, :], ACT.Identity,
                               scale=vec[:, 0:1], bias=vec[:, 1:2]).then_inc(xnT_ready, 1)

            for k in range(NG + 1):
                if k < NG:
                    act.wait_ge(agg_done, NG + k + 1)
                    if k >= SN:
                        act.wait_ge(tr_done, k - 1)
                    act.activation(hT[:, k % SN, :], ps[:, k, :], ACT.Copy).then_inc(accT_ready, 1)
                if k:
                    xnT_group(k - 1)
            act.wait_ge(wa_done, 1)
            act.activation(wa[:, :], ps[:, 0, 0:2 * K], ACT.Copy).then_inc(wa_ready, 1)
            act.wait_ge(st_done, 1)
            act.activation(st[:, :, :].rearrange("p b k -> p (b k)"), ps[:, 1, 0:B * 2 * K], ACT.Copy)\
                .then_inc(st_ready, 1)
            n = passes(act)

            def head_start(head):
                for k in range(NG):
                    act.wait_ge(h_done, head * NG + k + 1)
                    act.activation(h[:, group(k), :].rearrange("p b c -> p (b c)"), ps[:, k, :], ACT.Copy)\
                        .then_inc(h_ready, 1)
                for k in range(NG):
                    act.wait_ge(s_done, head * NG + k + 1)
                    act.activation(negs[:, cols(k, GW)], ps[:, k, :], ACT.Copy, scale=-1.0).then_inc(negs_ready, 1)

            def head_end(head):
                for k in range(NG + 1):
                    if k < NG:
                        act.wait_ge(att_t_done, head * NG + k + 1)
                        act.activation(tbuf[:, k % SN, :], ps[:, 2 * (k % 4), :], ACT.Identity,
                                       scale=vec[:, 2:3], bias=vec[:, 3:4]).then_inc(att_t_ready, 1)
                    if k:
                        m = head * NG + k - 1
                        act.wait_ge(y_done, m + 1)
                        if m:
                            act.wait_ge(elu_used, m)
                        y = ps[:, 2 * ((k - 1) % 4) + 1, :]
                        act.activation(tbuf[:, 2, :], y, ACT.Exp).then_inc(y_read, 1)
                        act.activation(tbuf[:, 3, :], y, ACT.Relu).then_inc(y_read, 1)

            head_start(0)
            for head in range(K):
                with act.Fori(n * head, n * (head + 1)) as q:
                    act.wait_ge(factors_ready, q + 1)
                    act.activation(uu[:, :], tm[0][:, :], ACT.Exp)
                    act.activation(vv[:, :], tm[0][:, :], ACT.Exp, scale=0.01)
                    act.activation(UU[:, :], tm[2][:, :], ACT.Exp)
                    act.activation(VV[:, :], tm[3][:, :], ACT.Exp).then_inc(exp_ready, 1)

                    def high_part(c):
                        for w in range(2):
                            act.wait_ge(prod_ready, q * (2 * NG) + (2 * c + w + 1))
                            act.activation(MV[w][:, group(c), 0:C], prod[w].rearrange("p (b c) -> p b c", c=C), ACT.Copy)\
                                .then_inc(hi_ready, 1)

                    def expand(g, c):
                        at = q * GC + g * NC + c
                        act.wait_ge(x_made, at * JC + (JC + X_CREDIT))
                        act.wait_ge(bank_done, at * BANKS + BANKS)
                        act.activation(PQ[:, c % SN, 1, :, :].rearrange("p b n -> p (b n)"),
                                       X[:, c % SN, :, :].rearrange("p b n -> p (b n)"), ACT.Relu,
                                       scale=-1.0, bias=small[:, 8:9]).then_inc(q_made, 1)

                    def scale_sums(g):
                        for ib in range(BPG):
                            gi = q * NG + g
                            act.wait_ge(num_added, gi * BPG + (ib + 1))
                            for w in range(2):
                                act.wait_ge(bank_done, gi * (NC * BANKS) + ((NC - 1) * BANKS + ib * 2 + w + 1 + DONE_CREDIT))
                                act.activation(ev[:, ib % SN, w, :], ps[:, ib * 2 + w, 0:MVW], ACT.Copy,
                                               scale=(UU, VV)[w][:, bass.ds(g * BPG + ib, 1)]).then_inc(ev_ready, 1)

                    high_part(0)
                    for c in range(NC):
                        if c + 1 < NC:
                            high_part(c + 1)
                        expand(0, c)
                    with act.Fori(1, NG) as g:
                        expand(g, 0)
                        scale_sums(g - 1)
                        for c in range(1, NC):
                            expand(g, c)
                    scale_sums(NG - 1)
                if head + 1 < K:
                    head_start(head + 1)
                head_end(head)

        @block.vector
        def _(v):
            steps = [0]

            def step(instruction):
                steps[0] += 1
                instruction.then_inc(dve_step, 1)
                v.wait_ge(dve_step, steps[0])

            v.sem_inc(rowsum_done, ROW_CREDIT)
            v.sem_inc(mask_made, MASK_CREDIT)
            v.sem_inc(x_made, X_CREDIT)
            v.sem_inc(p_made, PQ_CREDIT)
            v.memset(zeros[:, :], 0.0).then_inc(zeros_ready, 1)
            v.memset(small[:, 8:9], -1.0).then_inc(zeros_ready, 1)
            v.memset(mstar[:, :], 0.0).then_inc(zeros_ready, 1)
            v.wait_ge(ident_ready, 4)
            v.wait_ge(xw_ready, NG)
            DS = 5
            with v.Fori(0, NI) as i:
                for u in range(RING):
                    b = i * RING + u
                    v.wait_ge(row_loaded[u % 2], i * 32 + 16 * (u // 2 + 1))
                    v.tensor_reduce(part[:, :], rowbuf[:, u % 2, :].rearrange("p (a n) -> p a n", a=8), AX_X, ALU.add)\
                        .then_inc(rowsum_done, 1)
                    v.wait_ge(rowsum_done, b + (1 + ROW_CREDIT))
                    v.tensor_reduce(small[:, 0:1], part[:, :], AX_X, ALU.add).then_inc(deg_step, 1)
                    v.wait_ge(deg_step, b * DS + 1)
                    v.tensor_scalar(small[:, 1:2], small[:, 0:1], 1.0, TINY, ALU.add, ALU.max).then_inc(deg_ready, 1)
                    v.tensor_scalar(small[:, 2:3], small[:, 0:1], 1.0, 0.0, ALU.add, ALU.is_gt).then_inc(deg_step, 1)
                    v.wait_ge(deg_step, b * DS + 2)
                    v.wait_ge(pow_ready, b + 1)
                    d = d_all[:, bass.ds(b, 1)]
                    v.tensor_tensor(small[:, 4:5], small[:, 3:4], small[:, 2:3], ALU.mult).then_inc(deg_step, 1)
                    v.wait_ge(deg_step, b * DS + 3)
                    v.tensor_copy(d, small[:, 4:5]).then_inc(deg_step, 1)
                    v.tensor_tensor(small[:, 5:6], small[:, 4:5], small[:, 1:2], ALU.mult).then_inc(deg_step, 1)
                    v.wait_ge(deg_step, b * DS + 5)
                    v.wait_ge(pe_block, b + 1)
                    v.tensor_scalar(stat[:, u, :], block_of(xw_g, b), small[:, 4:5], None, ALU.mult)
                    v.tensor_scalar(diag[:, u, :], ident[:, :], small[:, 5:6], None, ALU.mult).then_inc(stat_ready, 1)
            step(v.tensor_tensor(d2_all[:, :], d_all[:, :], d_all[:, :], ALU.mult))
            for k in range(NG):
                v.wait_ge(hw_done, k + 1)
                v.tensor_tensor(xw_g[:, group(k), :], ps[:, k, :].rearrange("p (b c) -> p b c", c=C),
                                bcast(d2_all[:, group(k)], C), ALU.mult).then_inc(g_ready, 1)
            with v.Fori(0, NI) as i:
                for u in range(RING):
                    b = i * RING + u
                    v.wait_ge(col_loaded[u], i * 16 + 16 * (NI + 1))
                    v.wait_ge(mask_stored[u % SN], i * 32 + 16 * (u // SN + 1))
                    v.tensor_scalar(mtile[:, u % SN, :], colbuf[:, u, :], 0.0, 2.0, ALU.is_gt, ALU.mult)\
                        .then_inc(tile_step, 1)
                    v.wait_ge(tile_step, b + 1)
                    own = mtile[:, u % SN, bass.ds(b * P, P)]
                    v.tensor_tensor(own, own, ident2[:, :], ALU.max).then_inc(mask_made, 1)

            def norm(k, source, scale, ready=var_ready):
                for b in range(k * BPG, (k + 1) * BPG):
                    last = v.bn_stats(bn[:, b, :], source(b))
                step(last)
                for b in range(k * BPG, (k + 1) * BPG):
                    last = v.bn_aggr(mv[:, b, :], bn[:, b, :])
                step(last)
                v.tensor_scalar(scale[:, group(k)], mv[:, group(k), 1], LN_EPS, None, ALU.add).then_inc(ready, 1)

            v.wait_ge(xb2_ready, 1)
            for k in range(NG):
                v.wait_ge(tr_done, k + 1)
                for b in range(k * BPG, (k + 1) * BPG):
                    last = v.scalar_tensor_tensor(out=x1[:, b, :], in0=ps[:, k, cols(b % BPG)], scalar=d_all[:, b:b + 1],
                                                  in1=x1[:, b, :], op0=ALU.mult, op1=ALU.add)
                step(last)
                norm(k, lambda b: x1[:, b, :], rstd)
                v.wait_ge(rstd_ready, 2 * k + 1)
                for b in range(k * BPG, (k + 1) * BPG):
                    last = v.tensor_scalar(x1[:, b, :], x1[:, b, :], mv[:, b, 0:1], rstd[:, b:b + 1],
                                           ALU.subtract, ALU.mult)
                step(last)
                norm(k, lambda b: x1[:, b, :], r2)
                v.wait_ge(rstd_ready, 2 * k + 2)
                v.scalar_tensor_tensor(out=shift[:, group(k)], in0=mv[:, group(k), 0], scalar=-1.0, in1=r2[:, group(k)],
                                       op0=ALU.mult, op1=ALU.mult).then_inc(shift_ready, 1)

            v.wait_ge(st_ready, 1)
            for head in range(K):
                v.tensor_reduce(span[:, head:head + 1], st[:, :, 2 * head + 1], AX_X, ALU.max)
                last = v.tensor_reduce(span[:, K + head:K + head + 1], st[:, :, 2 * head + 1], AX_X, ALU.min)
            step(last)
            v.tensor_scalar(span[:, K:2 * K], span[:, K:2 * K], -1.0, None, ALU.mult).then_inc(span_ready, 1)
            v.wait_ge(top_ready, 1)
            step(v.tensor_tensor(npass_f[:, :], top[:, 0:K], top[:, K:2 * K], ALU.add))
            step(v.tensor_reduce(small[:, 6:7], npass_f[:, :], AX_X, ALU.max))
            step(v.tensor_scalar(small[:, 7:8], small[:, 6:7], 1.0 / WINDOW, 1.1, ALU.mult, ALU.add))
            v.tensor_copy(npass[:, :], small[:, 7:8]).then_inc(npass_ready, 1)
            n = passes(v)

            def source_column(head):
                if head:
                    v.wait_ge(s_done, head * NG)
                v.tensor_copy(was[:, :], wa[:, 2 * head:2 * head + 1].broadcast_to([P, P])).then_inc(was_ready, 1)

            def head_end(head):
                v.wait_ge(num_added, n * ((head + 1) * NG * BPG) + EV_CREDIT)
                v.tensor_copy(tm[0][:, :], num[:, :, C]).then_inc(dve_step, 1)
                steps[0] += 1
                v.wait_ge(dve_step, steps[0])
                step(v.reciprocal(tm[1][:, :], tm[0][:, :]))
                for k in range(NG + 1):
                    if k < NG:
                        for b in range(k * BPG, (k + 1) * BPG):
                            last = v.scalar_tensor_tensor(out=num[:, b, 0:C], in0=num[:, b, 0:C], scalar=tm[1][:, b:b + 1],
                                                          in1=x1[:, b, :], op0=ALU.mult, op1=ALU.add)
                        step(last)
                        norm(k, lambda b: num[:, b, 0:C], rstd)
                        v.wait_ge(rstd_ready, (2 + head) * NG + k + 1)
                        for b in range(k * BPG, (k + 1) * BPG):
                            last = v.tensor_scalar(num[:, b, 0:C], num[:, b, 0:C], mv[:, b, 0:1], rstd[:, b:b + 1],
                                                   ALU.subtract, ALU.mult)
                        last.then_inc(att_ready, 1)
                    if k:
                        m = head * NG + k - 1
                        acc_k = acc[:, group(k - 1), :].rearrange("p b c -> p (b c)")
                        base = (x1 if head == 0 else acc)[:, group(k - 1), :].rearrange("p b c -> p (b c)")
                        v.wait_ge(y_read, 2 * m + 2)
                        step(v.tensor_scalar(tbuf[:, 2, :], tbuf[:, 2, :], 1.0, -1.0, ALU.min, ALU.add))
                        step(v.tensor_tensor(tbuf[:, 2, :], tbuf[:, 2, :], tbuf[:, 3, :], ALU.add))
                        v.scalar_tensor_tensor(out=acc_k, in0=tbuf[:, 2, :], scalar=1.0 / K, in1=base,
                                               op0=ALU.mult, op1=ALU.add).then_inc(elu_used, 1)
                        if head == K - 1:
                            v.wait_ge(elu_used, m + 1)
                            norm(k - 1, lambda b: acc[:, b, :], r2, last_var_ready)
                            v.wait_ge(last_rstd_ready, k)
                            for b in range((k - 1) * BPG, k * BPG):
                                last = v.tensor_scalar(acc[:, b, :], acc[:, b, :], mv[:, b, 0:1], r2[:, b:b + 1],
                                                       ALU.subtract, ALU.mult)
                            last.then_inc(out_ready, 1)

            source_column(0)
            v.wait_ge(zeros_ready, 3)
            for head in range(K):
                t_col = 2 * head + 1
                step(v.tensor_copy(gref[:, 0:1], top[:, head:head + 1]))
                if head:
                    step(v.memset(mstar[:, :], 0.0))
                v.wait_ge(num_zeroed, head + 1)
                v.wait_ge(h_ready, (head + 1) * NG)
                v.wait_ge(negs_ready, (head + 1) * NG)
                with v.Fori(n * head, n * (head + 1)) as q:
                    done = [0]

                    def pstep(instruction):
                        done[0] += 1
                        instruction.then_inc(pass_step, 1)
                        v.wait_ge(pass_step, q * PASS_STEPS + done[0])

                    v.wait_ge(num_added, q * (NG * BPG) + EV_CREDIT)
                    v.wait_ge(bank_done, q * (GC * BANKS) + DONE_CREDIT)
                    src_s, src_t = st[:, :, 2 * head], st[:, :, t_col]
                    pstep(v.tensor_scalar(gref[:, 1:2], gref[:, 0:1], -WINDOW, None, ALU.add))
                    pstep(v.tensor_scalar(tm[0][:, :], src_t, gref[:, 0:1], 0.0, ALU.subtract, ALU.min))
                    pstep(v.tensor_scalar(tm[1][:, :], src_t, gref[:, 0:1], None, ALU.is_le))
                    pstep(v.scalar_tensor_tensor(out=tm[1][:, :], in0=src_t, scalar=gref[:, 1:2], in1=tm[1][:, :],
                                                 op0=ALU.is_gt, op1=ALU.mult))
                    pstep(v.tensor_scalar(tm[4][:, :], src_s, gref[:, 0:1], None, ALU.add))
                    pstep(v.scalar_tensor_tensor(out=tm[3][:, :], in0=tm[4][:, :], scalar=0.01, in1=tm[4][:, :],
                                                 op0=ALU.mult, op1=ALU.max))
                    pstep(v.tensor_scalar(tm[2][:, :], num[:, :, C], 0.0, None, ALU.is_gt))
                    pstep(v.tensor_tensor(mstar[:, :], mstar[:, :], tm[2][:, :], ALU.mult))
                    pstep(v.scalar_tensor_tensor(out=tm[3][:, :], in0=tm[2][:, :], scalar=1.0, in1=tm[3][:, :],
                                                 op0=ALU.subtract, op1=ALU.mult))
                    pstep(v.tensor_tensor(mstar[:, :], mstar[:, :], tm[3][:, :], ALU.subtract))
                    pstep(v.tensor_tensor(tm[2][:, :], tm[4][:, :], mstar[:, :], ALU.subtract))
                    v.scalar_tensor_tensor(out=tm[3][:, :], in0=tm[4][:, :], scalar=0.01, in1=mstar[:, :],
                                           op0=ALU.mult, op1=ALU.subtract).then_inc(factors_ready, 1)
                    v.wait_ge(exp_ready, q + 1)
                    for w, f in enumerate((uu, vv)):
                        low = MV[w][:, :, MVW - 1]
                        pstep(v.tensor_tensor(f[:, :], f[:, :], tm[1][:, :], ALU.mult))
                        pstep(v.tensor_copy(MV[w][:, :, C], f[:, :]))
                        pstep(v.tensor_tensor(low, f[:, :], MV[w][:, :, C].bitcast(F32), ALU.subtract))
                    pstep(v.tensor_copy(gref[:, 0:1], gref[:, 1:2]))
                    assert done[0] == PASS_STEPS

                    def product(c):
                        if c:
                            v.wait_ge(mv_ready, q * (2 * NG) + 2 * c)
                        for w, f in enumerate((uu, vv)):
                            v.tensor_tensor(prod[w].rearrange("p (b c) -> p b c", c=C), h[:, group(c), :],
                                            bcast(f[:, group(c)], C), ALU.mult).then_inc(prod_ready, 1)

                    def low_part(c):
                        for w in range(2):
                            v.wait_ge(hi_ready, q * (2 * NG) + (2 * c + w + 1))
                            v.tensor_tensor(MV[w][:, group(c), C + 1:MVW - 1], prod[w].rearrange("p (b c) -> p b c", c=C),
                                            MV[w][:, group(c), 0:C].bitcast(F32), ALU.subtract).then_inc(mv_ready, 1)

                    def chunk(g, c):
                        at = q * GC + g * NC + c
                        s = c % SN
                        v.wait_ge(mask_loaded[s], q * (8 * GC) + g * (8 * NC) + 16 * (c // SN + 1))
                        v.wait_ge(q_made, at + 1)
                        v.wait_ge(p_made, at + 1)
                        for j in range(JC):
                            v.scalar_tensor_tensor(out=X[:, s, j, :], in0=negs[:, bass.ds(g * GW, GW)],
                                                   scalar=st[:, c * JC + j, t_col:t_col + 1], in1=mring[:, s, j, :],
                                                   op0=ALU.is_le, op1=ALU.subtract).then_inc(x_made, 1)
                        v.wait_ge(bank_done, at * BANKS + BANKS)
                        for j in (0, 2):
                            v.wait_ge(x_made, at * JC + (j + 2 + X_CREDIT))
                            last = v.tensor_scalar(PQ[:, s, 0, j:j + 2, :].rearrange("p b n -> p (b n)"),
                                                   X[:, s, j:j + 2, :].rearrange("p b n -> p (b n)"),
                                                   -1.0, None, ALU.is_equal)
                        last.then_inc(p_made, 1)

                    product(0)
                    for c in range(NC):
                        low_part(c)
                        if c + 1 < NC:
                            product(c + 1)
                        chunk(0, c)
                    with v.Fori(1, NG) as g:
                        for c in range(NC):
                            chunk(g, c)
                if head + 1 < K:
                    source_column(head + 1)
                head_end(head)

        @block.tensor
        def _(pe):
            def multiply(*args, **kw):
                return pe.matmul(*args, skip_group_check=True, **kw)

            def zero_banks(start, stop, k):
                return multiply(ps[:, k, :], zeros[:, 0:P], zeros[:, :], start=start, stop=stop)

            def aggregate(i, u, extra):
                for k in range(NG):
                    multiply(ps[:, k, :], stat[:, u, :], colbuf[:, u, cols(k, GW)], start=False, stop=False)
                own = ps[:, bass.ds(i, 1), cols(u)].rearrange("p o n -> p (o n)")
                last = multiply(own, stat[:, u, :], ident[:, :], start=False, stop=False)
                if extra:
                    last = multiply(own, b1bc[:, :], diag[:, u, :], start=False, stop=False)
                last.then_inc(pe_block, 1)

            pe.sem_inc(pe_block, COL_CREDIT)
            pe.sem_inc(bank_done, DONE_CREDIT)
            pe.wait_ge(consts, ALL_CONSTS)
            for k in range(NG):
                for b in range(k * BPG, (k + 1) * BPG):
                    last = multiply(ps[:, k, cols(b % BPG)], xnT[:, cols(b)], w1[:, :], start=True, stop=True)
                last.then_inc(xw_done, 1)
            pe.wait_ge(zeros_ready, 3)
            for k in range(NG):
                pe.wait_ge(xw_ready, k + 1)
                zero_banks(True, False, k)
            with pe.Fori(0, NI) as i:
                for u in range(RING):
                    pe.wait_ge(col_loaded[u], i * 16 + 16)
                    pe.wait_ge(stat_ready, i * RING + (u + 1))
                    aggregate(i, u, True)
            for k in range(NG):
                zero_banks(False, True, k).then_inc(agg_done, 1)
            for k in range(NG):
                pe.wait_ge(hT_ready, k + 1)
                for ib in range(BPG):
                    last = multiply(ps[:, k, cols(ib)], hT[:, k % SN, cols(ib)], w2[:, :], start=True, stop=True)
                last.then_inc(hw_done, 1)
            for k in range(NG):
                pe.wait_ge(g_ready, k + 1)
                zero_banks(True, False, k)
            with pe.Fori(0, NI) as i:
                for u in range(RING):
                    pe.wait_ge(col_loaded[u], i * 16 + 16 * (NI + 1))
                    pe.wait_ge(g_copied, i * RING + (u + 1))
                    aggregate(i, u, False)
            for k in range(NG):
                zero_banks(False, True, k).then_inc(agg_done, 1)
            for k in range(NG + 1):
                if k < NG:
                    pe.wait_ge(accT_ready, k + 1)
                    for ib in range(BPG):
                        last = pe.transpose(ps[:, k, cols(ib)], hT[:, k % SN, cols(ib)], ident[:, :])
                    last.then_inc(tr_done, 1)
                if k:
                    pe.wait_ge(xn_ready, k * BPG)
                    for ib in range(BPG):
                        last = pe.transpose(ps[:, k - 1, cols(ib)], h[:, (k - 1) * BPG + ib, :], ident[:, :])
                    last.then_inc(xnt_done, 1)
            pe.wait_ge(xnT_ready, NG)
            for head in range(K):
                last = multiply(ps[:, 0, cols(head, 2)], ff0[:, head, :], attnT[:, head, :], start=True, stop=True)
            last.then_inc(wa_done, 1)
            pe.wait_ge(wa_ready, 1)
            for b in range(B):
                last = multiply(ps[:, 1, cols(b, 2 * K)], xnT[:, cols(b)], wa[:, :], start=True, stop=True)
            last.then_inc(st_done, 1)
            pe.wait_ge(st_ready, 1)
            n = passes(pe)

            def head_start(head):
                for k in range(NG):
                    if head:
                        pe.wait_ge(ev_ready, n * (head * NG * 8) + BANK_CREDIT)
                    for ib in range(BPG):
                        last = multiply(ps[:, k, cols(ib)], xnT[:, cols(k * BPG + ib)], ff0T[:, head, :],
                                        start=True, stop=True)
                    last.then_inc(h_done, 1)
                pe.wait_ge(was_ready, head + 1)
                for k in range(NG):
                    pe.wait_ge(h_ready, head * NG + k + 1)
                    multiply(ps[:, k, :], was[:, :], xnT[:, cols(k, GW)], start=True, stop=True).then_inc(s_done, 1)
                pe.wait_ge(negs_ready, (head + 1) * NG)

            head_start(0)
            for head in range(K):
                with pe.Fori(n * head, n * (head + 1)) as q:
                    with pe.Fori(0, NG) as g:
                        for c in range(NC):
                            at = q * GC + g * NC + c
                            pe.wait_ge(mv_ready, q * (2 * NG) + (2 * c + 2))
                            pe.wait_ge(p_made, at + (1 + PQ_CREDIT))
                            pe.wait_ge(q_made, at + (1 + PQ_CREDIT))
                            for bank in range(BANKS):
                                ib, w = bank // 2, bank % 2
                                if c == 0:
                                    pe.wait_ge(ev_ready, (q * NG + g) * 8 + (bank + 1))
                                for j in range(JC):
                                    last = multiply(ps[:, bank, 0:MVW], PQ[:, c % SN, w, j, cols(ib)],
                                                    MV[w][:, c * JC + j, :],
                                                    start=c == 0 and j == 0, stop=c == NC - 1 and j == JC - 1)
                                last.then_inc(bank_done, 1)
                if head + 1 < K:
                    head_start(head + 1)
                for k in range(NG + 1):
                    if k < NG:
                        m = head * NG + k
                        pe.wait_ge(att_ready, m + 1)
                        if k >= 4:
                            pe.wait_ge(att_t_ready, m - 3)
                        for ib in range(BPG):
                            last = pe.transpose(ps[:, 2 * (k % 4), cols(ib)], num[:, k * BPG + ib, 0:C], ident[:, :])
                        last.then_inc(att_t_done, 1)
                    if k:
                        m = head * NG + k - 1
                        pe.wait_ge(att_t_ready, m + 1)
                        if k > 4:
                            pe.wait_ge(y_read, 2 * (m - 4) + 2)
                        for ib in range(BPG):
                            last = multiply(ps[:, 2 * ((k - 1) % 4) + 1, cols(ib)], tbuf[:, (k - 1) % SN, cols(ib)],
                                            ff1T[:, head, :], start=True, stop=True)
                        last.then_inc(y_done, 1)
                if head + 1 < K:
                    pe.wait_ge(y_read, 2 * (head + 1) * NG)


_INS = ["x", "xT", "adj", "adjT", "W1", "b1", "W2", "b2", "ff0", "ff0T", "ff1T", "attnT",
        "ln1_g", "ln1_b", "ln2_g", "ln2_b"]


def kernel(x, adj, L0_gnn_W1, L0_gnn_b1, L0_gnn_W2, L0_gnn_b2, L1_gnn_ff0_w, L1_gnn_ff1_w, L1_gnn_attn_w,
           L1_gnn_g1, L1_gnn_b1, L1_gnn_g2, L1_gnn_b2):
    import numpy as np
    from concourse import bacc
    from concourse.bass_utils import run_bass_kernel_spmd

    ff0, ff1, attn = np.asarray(L1_gnn_ff0_w), np.asarray(L1_gnn_ff1_w), np.asarray(L1_gnn_attn_w)
    heads, c = ff0.shape[0], ff0.shape[1]
    given = {
        "x": x, "xT": np.asarray(x).T, "adj": adj, "adjT": np.asarray(adj).T,
        "W1": L0_gnn_W1, "b1": L0_gnn_b1, "W2": L0_gnn_W2, "b2": L0_gnn_b2,
        "ff0": ff0, "ff0T": ff0.transpose(0, 2, 1), "ff1T": ff1.transpose(0, 2, 1),
        "attnT": attn.reshape(heads, 2, c).transpose(2, 0, 1),
        "ln1_g": L1_gnn_g1, "ln1_b": L1_gnn_b1, "ln2_g": L1_gnn_g2, "ln2_b": L1_gnn_b2,
    }
    arrays = {name: np.ascontiguousarray(given[name]) for name in _INS}
    nc = bacc.Bacc("TRN2", target_bir_lowering=False, num_devices=1)
    t = {name: nc.dram_tensor(f"in_{name}", arrays[name].shape, F32, kind="ExternalInput").ap() for name in _INS}
    out = nc.dram_tensor("out", arrays["x"].shape, F32, kind="ExternalOutput").ap()
    build(nc, t, out)
    r = run_bass_kernel_spmd(nc, [{f"in_{name}": a for name, a in arrays.items()}], core_ids=[0])
    return r.results[0]["out"]
```

```python
from contextlib import ExitStack

import concourse.bass as bass
from concourse import mybir

F32 = mybir.dt.float32
F32R = mybir.dt.float32r
BF16 = mybir.dt.bfloat16
U8 = mybir.dt.uint8
I32 = mybir.dt.int32
ALU = mybir.AluOpType
ACT = mybir.ActivationFunctionType
AX_X = mybir.AxisListType.X

P = 128
GW = 512
BPG = GW // P
JC = 4
RING = 4
SLOPE = 0.01
WINDOW = 48.0
LN_EPS = 1e-5
TINY = 1e-30


def bcast(column, n):
    return column.unsqueeze(2).broadcast_to([column.shape[0], column.shape[1], n])


def build(nc, t, out):
    N, C = t["x"].shape
    K = t["ff0"].shape[0]
    B = N // P
    NG = N // GW
    NC = B // JC
    NI = B // RING
    SN = 2
    TS = min(4, NC)
    assert C == P and K == 2 and NG <= 8 and NC == NG and B * JC >= 2 * RING

    mask_dram = nc.dram_tensor("mask_by_group", [NG, P, B, GW], U8).ap()

    ctx = ExitStack()
    with ctx:
        block_scope = ctx

        def sb(name, shape, dtype, scope=None):
            return (scope or block_scope).enter_context(nc.sbuf_tensor(name, shape, dtype))

        def sem(name):
            return block_scope.enter_context(nc.semaphore(name))

        x1 = sb("x1", [P, B, C], F32)
        xnT_acc = sb("xnT_acc", [P, B, C], F32)
        ident = sb("ident", [P, P], F32)
        ident_u8 = sb("ident_u8", [P, P], U8)
        zeros = sb("zeros", [P, GW], BF16)
        mean = sb("mean", [P, P], F32)
        w1 = sb("w1", [P, C], F32)
        w2 = sb("w2", [P, C], F32)
        b1bc = sb("b1bc", [P, C], F32)
        b2bc = sb("b2bc", [P, C], F32)
        vec = sb("vec", [P, 5], F32)
        ff0 = sb("ff0", [P, K, C], F32)
        ff0T = sb("ff0T", [P, K, C], F32)
        turn = sb("turn", [P, P], F32)
        fold = sb("fold", [P, K, C], F32)
        ff1T = sb("ff1T", [P, K, C], F32)
        attnT = sb("attnT", [P, K, 2], F32)
        wa = sb("wa", [P, K * 2], F32)
        was = sb("was", [P, K, P], F32)
        half = sb("half", [P, B], F32)
        d_all = sb("d_all", [P, B], F32)
        d2_all = sb("d2_all", [P, B], F32)
        small = sb("small", [P, 16], F32)
        bn = sb("bn", [P, 2, B, 6], F32)
        mv = sb("mv", [P, 2, B, 2], F32)
        rstd = sb("rstd", [P, B], F32)
        r2 = sb("r2", [P, B], F32)
        shift = sb("shift", [P, B], F32)
        st = sb("st", [P, B, K * 2], F32)
        span = sb("span", [P, 2 * K], F32)
        top = sb("top", [P, 2 * K], F32)
        npass_f = sb("npass_f", [P, 2], F32)
        npass = sb("npass", [P, 1], I32)
        gref = sb("gref", [P, 2], F32)
        below = sb("below", [P, B], F32)
        inside = sb("inside", [P, B], F32)
        ratio = sb("ratio", [P, B], F32)
        weight = sb("weight", [P, B], F32)
        inv_den = sb("inv_den", [P, B], F32)
        node_den = sb("node_den", [P, BPG], F32)
        r2w = sb("r2w", [P, B], F32)

        first = ExitStack()
        rowbuf = sb("rowbuf", [P, 2, N], F32, first)
        colbuf = sb("colbuf", [P, RING, N], F32, first)
        xw_g = sb("xw_g", [P, B, C], F32, first)
        mtile = sb("mtile", [P, 2, N], U8, first)
        stat = sb("stat", [P, RING, C], F32, first)
        diag = sb("diag", [P, RING, C], F32, first)
        hT = sb("hT", [P, 2, GW], F32, first)
        part = sb("part", [P, 8], F32, first)
        first.close()

        Yw = sb("Yw", [P, B, C], F32)
        srow = sb("srow", [P, K, N], F32)
        Rrow = sb("Rrow", [P, N], F32)
        ref = sb("ref", [P, N], F32)
        den = sb("den", [P, N], F32)
        num = sb("num", [P, N], F32)
        T = sb("T", [P, TS, JC, GW], F32)
        mring = sb("mring", [P, TS, JC, GW], U8)
        log_scale = sb("log_scale", [P, GW], F32)
        above = sb("above", [P, GW], F32)
        scale_row = sb("scale_row", [P, GW], F32)
        scaled = sb("scaled", [P, GW], F32)
        tbuf = T[:, :, :, :].rearrange("p a b c -> p (a b) c")

        ps = ctx.enter_context(nc.psum_tensor("ps", [P, 8, GW], F32))


        def sems(names):
            return [sem(name) for name in names.split()]

        xT_loaded = [sem(f"xT_loaded{k}") for k in range(NG)]
        first_loaded, consts, ident_ready, zeros_ready, xb2_ready = sems("first_loaded consts ident_ready zeros_ready xb2_ready")
        row_loaded = sems("row_loaded0 row_loaded1")
        col_loaded = [sem(f"col_loaded{s}") for s in range(RING)]
        mask_stored = sems("mask_stored0 mask_stored1")
        mask_loaded = [sem(f"mask_loaded{s}") for s in range(TS)]
        xw_done, xw_ready, rowsum_done, deg_step, deg_ready, pow_ready = sems(
            "xw_done xw_ready rowsum_done deg_step deg_ready pow_ready")
        stat_ready, pe_block, agg_done, hT_ready, hw_done, g_ready, g_copied, mask_made, tile_step = sems(
            "stat_ready pe_block agg_done hT_ready hw_done g_ready g_copied mask_made tile_step")
        dve_step, accT_ready, tr_done, shift_ready, xn_ready, xnt_done, xnT_ready = sems(
            "dve_step accT_ready tr_done shift_ready xn_ready xnt_done xnT_ready")
        weights_done, weights_read, st_done, st_ready, span_ready, top_ready, npass_ready, was_ready = sems(
            "weights_done weights_read st_done st_ready span_ready top_ready npass_ready was_ready")
        s_done, srow_ready, sums_zeroed, pass_step, below_ready, exp_ready, rows_clamped, R_ready, yw_ready = sems(
            "s_done srow_ready sums_zeroed pass_step below_ready exp_ready rows_clamped R_ready yw_ready")
        relu_made, t_made, chunk_done, row_step, scale_row_ready, sum_step, num_ready, den_done, den_read = sems(
            "relu_made t_made chunk_done row_step scale_row_ready sum_step num_ready den_done den_read")
        mean_ready, turn_ready, den_step, att_h_done, att_ready, att_t_done, att_t_ready, y_done, y_read = sems(
            "mean_ready turn_ready den_step att_h_done att_ready att_t_done att_t_ready y_done y_read")
        out_ready, stored, loads_started, gref_moved, relus_started = sems("out_ready stored loads_started gref_moved relus_started")

        LAST = K + 1
        rows_ready, stats_ready, moments_ready, scale_ready = (
            [sem(f"{what}{z}") for z in range(K + 2)]
            for what in ("rows_ready", "stats_ready", "moments_ready", "scale_ready"))
        x1_ready, r2_ready, elu_ready, acc_added, pool_step = sems("x1_ready r2_ready elu_ready acc_added pool_step")

        adj_rows = t["adj"].rearrange("(b p) n -> b p n", p=P)
        adj_cols = t["adjT"].rearrange("(b p) n -> b p n", p=P)
        out_v = out.rearrange("(b p) c -> p b c", p=P)
        xnT = xnT_acc[:, :, :].rearrange("p b c -> p (b c)")
        acc = xnT_acc

        def block_of(tensor, b):
            return tensor[:, bass.ds(b, 1), :].rearrange("p o n -> p (o n)")

        def row_of(tensor, g):
            return tensor[:, bass.ds(g * GW, GW)]

        def bank(g):
            return ps[:, bass.ds(g, 1), :].rearrange("p o n -> p (o n)")

        def dram_block(tensor, b):
            return tensor[bass.ds(b, 1), :, :].rearrange("o p n -> (o p) n")

        def group(k):
            return slice(k * BPG, (k + 1) * BPG)

        def cols(k, n=P):
            return slice(k * n, (k + 1) * n)

        FIRST = [(w1[:, :], t["W1"]), (b1bc[:, :], t["b1"].partition_broadcast(P))]
        CONSTS = [
            (w2[:, :], t["W2"]), (b2bc[:, :], t["b2"].partition_broadcast(P)),
            (ff0[:, :, :], t["ff0"].rearrange("k o i -> o k i")),
            (ff0T[:, :, :], t["ff0T"].rearrange("k i o -> i k o")),
            (ff1T[:, :, :], t["ff1T"].rearrange("k i o -> i k o")),
            (attnT[:, :, :], t["attnT"]),
            (x1[:, :, :], t["x"].rearrange("(b p) c -> p b c", p=P)),
        ] + [(vec[:, m:m + 1], t[name].rearrange("(p o) -> p o", o=1))
             for m, name in enumerate(("ln1_g", "ln1_b", "ln2_g", "ln2_b"))]
        ALL_CONSTS = 16 * len(CONSTS)
        ALL_FIRST = 16 * len(FIRST)

        ROW_CREDIT, COL_CREDIT = 2, RING
        STORE_CREDIT = 16
        MASK_CREDIT = B + COL_CREDIT
        GC = NG * NC
        PASS_STEPS = 5
        ROW_STEPS = 5
        USES = [sum(c % TS == s for c in range(NC)) for s in range(TS)]
        MAX_PASSES = 1 << 12
        STATS, MOMENTS, SHIFT = 1, 2, 3
        LATE = 2
        TURN = SHIFT + 1
        ELU = 7
        END = ELU + 1 + 1 + 1

        def passes(eng):
            eng.wait_ge(npass_ready, 1)
            return eng.value_load(npass[0:1, 0:1], min_val=1, max_val=MAX_PASSES)

        block = ctx.enter_context(nc.Block())

        @block.sync
        def _(sp):
            with sp.Fori(0, NI) as i:
                for u in range(RING):
                    b = i * RING + u
                    sp.wait_ge(rowsum_done, b + 1)
                    sp.dma_start(rowbuf[:, u % 2, :], dram_block(adj_rows, b)).then_inc(row_loaded[u % 2], 16)
                    sp.wait_ge(pe_block, b + 1)
                    sp.dma_start(colbuf[:, u, :], dram_block(adj_cols, b)).then_inc(col_loaded[u], 16)
            with sp.Fori(0, NI) as i:
                for u in range(RING):
                    b = i * RING + u
                    sp.wait_ge(pe_block, b + B + 1)
                    sp.wait_ge(mask_made, b + B + 1)
                    sp.dma_start(colbuf[:, u, :], dram_block(adj_cols, b)).then_inc(col_loaded[u], 16)
            for s in range(SN):
                sp.wait_ge(mask_stored[s], 16 * (B // SN) + STORE_CREDIT)
            n = passes(sp)
            with sp.Fori(0, n * K) as q:
                with sp.Fori(0, NG) as g:
                    for c in range(NC):
                        sp.wait_ge(t_made, q * GC + g * NC + (c + 1))
                        sp.sem_inc(loads_started, 1)
                        sp.dma_start(mring[:, c % TS, :, :],
                                     mask_dram[bass.ds(g, 1), :, cols(c, JC), :].rearrange("o p b n -> (o p) b n"))\
                            .then_inc(mask_loaded[c % TS], 16)
            for k in range(NG):
                sp.wait_ge(out_ready, k + 1)
                sp.dma_start(out_v[:, group(k), :], acc[:, group(k), :]).then_inc(stored, 16)
            sp.wait_ge(stored, 16 * NG)

        @block.gpsimd
        def _(pool):
            pool.memset(ident[:, :], 0.0).then_inc(ident_ready, 1)
            pool.memset(half[:, :], -0.5).then_inc(ident_ready, 1)
            pool.wait_ge(ident_ready, 2)
            pool.affine_select(out=ident[:, :], in_=ident[:, :], compare_op=ALU.not_equal, fill=1.0, base=0,
                               pattern=[[-1, P]], channel_multiplier=1).then_inc(ident_ready, 1)
            pool.wait_ge(ident_ready, 3)
            pool.tensor_copy(ident_u8[:, :], ident[:, :]).then_inc(ident_ready, 1)
            pool.memset(mean[:, :], 1.0 / C).then_inc(mean_ready, 1)
            with pool.Fori(0, B) as b:
                pool.wait_ge(deg_ready, b + 1)
                pool.tensor_tensor(small[:, 3:4], small[:, 1:2], half[:, 0:1], ALU.pow).then_inc(pow_ready, 1)
            pool.wait_ge(consts, ALL_CONSTS)
            pool.tensor_tensor(x1[:, :, :], x1[:, :, :], b2bc[:, :].unsqueeze(1).broadcast_to([P, B, C]), ALU.add)\
                .then_inc(xb2_ready, 1)
            done = [0]

            def pstep(instruction):
                done[0] += 1
                instruction.then_inc(pool_step, 1)
                pool.wait_ge(pool_step, done[0])

            def norm_scale(z, k, scale):
                pool.wait_ge(moments_ready[z], k + 1)
                pstep(pool.tensor_scalar(scale[:, group(k)], mv[:, z // LAST, group(k), 1], LN_EPS, 1.0, ALU.add, ALU.mult))
                pool.tensor_tensor(scale[:, group(k)], scale[:, group(k)], half[:, group(k)], ALU.pow)\
                    .then_inc(scale_ready[z], 1)

            for k in range(NG):
                norm_scale(0, k, rstd)
                pool.wait_ge(scale_ready[0], k + 1)
                r = r2[:, group(k)]
                pstep(pool.tensor_tensor(r, rstd[:, group(k)], rstd[:, group(k)], ALU.mult))
                pstep(pool.tensor_tensor(r, r, mv[:, 0, group(k), 1], ALU.mult))
                pstep(pool.tensor_scalar(r, r, LN_EPS, 1.0, ALU.add, ALU.mult))
                pool.tensor_tensor(r, r, half[:, group(k)], ALU.pow).then_inc(r2_ready, 1)
            pool.wait_ge(span_ready, 1)
            pool.partition_all_reduce(top[:, :], span[:, :], P, bass.bass_isa.ReduceOp.max).then_inc(top_ready, 1)
            pool.memset(ref[:, :], 0.0).then_inc(sums_zeroed, 1)
            pool.memset(den[:, :], 0.0).then_inc(sums_zeroed, 1)
            pool.memset(num[:, :], 0.0).then_inc(sums_zeroed, 1)
            for head in range(K):
                if head + 1 < K:
                    pool.wait_ge(rows_ready[1 + head], 1)
                    pool.memset(den[:, :], 0.0).then_inc(sums_zeroed, 1)
                for i in range(NG + END):
                    k = i - MOMENTS
                    if 0 <= k < NG:
                        norm_scale(1 + head, k, rstd)
                    if k == NG - 1 and head + 1 < K:
                        pool.wait_ge(att_h_done, (head + 1) * NG)
                        pool.memset(num[:, :], 0.0).then_inc(sums_zeroed, 1)
                    k = i - ELU
                    if 0 <= k < NG:
                        m = head * NG + k
                        base = (x1 if head == 0 else acc)[:, group(k), :].rearrange("p b c -> p (b c)")
                        pool.wait_ge(elu_ready, m + 1)
                        pool.tensor_tensor(acc[:, group(k), :].rearrange("p b c -> p (b c)"), base, tbuf[:, 2 + k % SN, :],
                                           ALU.add).then_inc(acc_added, 1)
                    k = i - ELU - 1 - 1
                    if 0 <= k < NG and head == K - 1:
                        norm_scale(LAST, k, r2)

        @block.scalar
        def _(act):
            for dst, src in FIRST:
                act.dma_start(dst, src).then_inc(first_loaded, 16)
            for k in range(NG):
                act.dma_start(xnT[:, cols(k, GW)], t["xT"][:, cols(k, GW)]).then_inc(xT_loaded[k], 16)
            act.sem_inc(relu_made, 1)
            act.sem_inc(den_read, NG)
            for s in range(SN):
                act.sem_inc(mask_stored[s], STORE_CREDIT)
            for k in range(NG):
                act.wait_ge(xw_done, k + 1)
                act.activation(xw_g[:, group(k), :].rearrange("p b c -> p (b c)"), ps[:, k, :], ACT.Copy)\
                    .then_inc(xw_ready, 1)
            for dst, src in CONSTS:
                act.dma_start(dst, src).then_inc(consts, 16)
            for k in range(NG):
                act.wait_ge(agg_done, k + 1)
                if k >= SN:
                    act.wait_ge(hw_done, k - 1)
                act.activation(hT[:, k % SN, :], ps[:, k, :], ACT.Relu).then_inc(hT_ready, 1)
            act.wait_ge(weights_done, 1)
            act.activation(fold[:, :, :].rearrange("p k c -> p (k c)"), ps[:, 0, 0:K * C], ACT.Copy)\
                .then_inc(weights_read, 1)
            act.activation(wa[:, :], ps[:, 0, K * C:K * (C + 2)], ACT.Copy).then_inc(weights_read, 1)
            act.wait_ge(g_ready, NG)
            with act.Fori(0, NI) as i:
                for u in range(RING):
                    b = i * RING + u
                    act.wait_ge(pe_block, b + B + 1)
                    act.activation(stat[:, u, :], block_of(xw_g, b), ACT.Copy).then_inc(g_copied, 1)
                    act.wait_ge(mask_made, b + (1 + MASK_CREDIT))
                    act.dma_start(mask_dram[:, :, bass.ds(b, 1), :].rearrange("g p o n -> p g (o n)"),
                                  mtile[:, u % SN, :].rearrange("p (g n) -> p g n", n=GW))\
                        .then_inc(mask_stored[u % SN], 16)

            def source_row(head, k, at):
                act.wait_ge(s_done, head * NG + k + 1)
                act.activation(srow[:, head, cols(k, GW)], ps[:, at, :], ACT.Copy).then_inc(srow_ready, 1)

            for i in range(NG + TURN + 4):
                k = i
                if k < NG:
                    act.wait_ge(agg_done, NG + k + 1)
                    if k >= SN:
                        act.wait_ge(tr_done, k - 1)
                    act.activation(hT[:, k % SN, :], ps[:, k, :], ACT.Copy).then_inc(accT_ready, 1)
                k = i - TURN
                if 0 <= k < NG:
                    act.wait_ge(x1_ready, k + 1)
                    act.wait_ge(r2_ready, k + 1)
                    for b in range(k * BPG, (k + 1) * BPG):
                        act.activation(Yw[:, b, :], x1[:, b, :], ACT.Copy, scale=r2[:, b:b + 1]).then_inc(xn_ready, 1)
                k = i - TURN - 1
                if 0 <= k < NG:
                    act.wait_ge(xnt_done, k + 1)
                    act.activation(xnT[:, cols(k, GW)], ps[:, k, :], ACT.Identity,
                                   scale=vec[:, 0:1], bias=vec[:, 1:2]).then_inc(xnT_ready, 1)
                k = i - TURN - 2
                if 0 <= k < NG:
                    act.wait_ge(st_done, k + 1)
                    act.activation(st[:, group(k), :].rearrange("p b k -> p (b k)"), ps[:, k, 0:BPG * 2 * K], ACT.Copy)\
                        .then_inc(st_ready, 1)
                k = i - TURN - 3
                if 0 <= k < NG:
                    source_row(0, k, k)

            def head_end(head):
                for i in range(NG + SHIFT + 3):
                    k = i - SHIFT - 2
                    if 0 <= k < NG:
                        m = head * NG + k
                        act.wait_ge(att_t_done, m + 1)
                        if k >= SN:
                            act.wait_ge(y_done, m - 1)
                        act.activation(tbuf[:, k % SN, :], ps[:, 4 + k % SN, :], ACT.Identity,
                                       scale=vec[:, 2:3], bias=vec[:, 3:4]).then_inc(att_t_ready, 1)
                    k = i - SHIFT - 3
                    if 0 <= k < NG:
                        m = head * NG + k
                        act.wait_ge(y_done, m + 1)
                        if k >= SN:
                            act.wait_ge(acc_added, m - 1)
                        y = ps[:, 6 + k % SN, :]
                        act.activation(tbuf[:, 2 + k % SN, :], y, ACT.Exp).then_inc(y_read, 1)
                        act.activation(tbuf[:, 4 + k % SN, :], y, ACT.Relu, scale=1.0 / K).then_inc(y_read, 1)
                    k = i - STATS - 1
                    if 0 <= k < NG and head + 1 < K:
                        source_row(head + 1, k, k % 4)
                    k = i - SHIFT
                    if 0 <= k < NG:
                        act.wait_ge(shift_ready, head * NG + k + 1)
                        for b in range(k * BPG, (k + 1) * BPG):
                            act.activation(Yw[:, b, :], Yw[:, b, :], ACT.Identity, scale=rstd[:, b:b + 1],
                                           bias=shift[:, b:b + 1]).then_inc(att_ready, 1)

            for s in range(SN):
                act.wait_ge(mask_stored[s], 16 * (B // SN) + STORE_CREDIT)
            n = passes(act)
            for head in range(K):
                with act.Fori(n * head, n * (head + 1)) as q:
                    act.wait_ge(below_ready, q + 1)
                    act.activation(ratio[:, :], below[:, :], ACT.Exp, scale=1.0 - SLOPE)
                    act.activation(weight[:, :], below[:, :], ACT.Exp, scale=SLOPE).then_inc(exp_ready, 1)
                    act.wait_ge(exp_ready, q + 1)

                    def exp_row(k):
                        act.wait_ge(rows_clamped, q * NG + (k + 1))
                        act.activation(Rrow[:, cols(k, GW)], Rrow[:, cols(k, GW)], ACT.Exp, scale=1.0 - SLOPE)\
                            .then_inc(R_ready, 1)

                    def relus(g, c):
                        at = q * GC + g * NC + c
                        act.wait_ge(chunk_done, at + 1)
                        if c == 0:
                            act.wait_ge(R_ready, q * NG + (g + 1))
                        act.sem_inc(relus_started, 1)
                        for j in range(JC):
                            last = act.activation(T[:, c % TS, j, :], row_of(Rrow, g), ACT.Relu,
                                                  scale=ratio[:, c * JC + j:c * JC + j + 1], bias=small[:, 8:9])
                        last.then_inc(relu_made, 1)

                    def exp_scale(g):
                        act.wait_ge(row_step, (q * NG + g) * ROW_STEPS + 4)
                        act.activation(scale_row[:, :], above[:, :], ACT.Exp, scale=-1.0).then_inc(scale_row_ready, 1)

                    def sums_to_den(g):
                        act.wait_ge(den_done, q * NG + (g + 1))
                        act.activation(row_of(den, g), bank(g), ACT.Copy).then_inc(den_read, 1)

                    exp_row(0)
                    if head:
                        act.wait_ge(acc_added, head * NG)
                    for c in range(NC):
                        relus(0, c)
                        if c + 1 < NG:
                            exp_row(c + 1)
                    with act.Fori(1, NG) as g:
                        for c in range(NC):
                            relus(g, c)
                            if c == min(1, NC - 1):
                                exp_scale(g - 1)
                            if c == NC - 1:
                                sums_to_den(g - 1)
                    exp_scale(NG - 1)
                    sums_to_den(NG - 1)
                head_end(head)

        @block.vector
        def _(v):
            steps = [0]

            def step(instruction):
                steps[0] += 1
                instruction.then_inc(dve_step, 1)
                v.wait_ge(dve_step, steps[0])

            v.sem_inc(rowsum_done, ROW_CREDIT)
            v.sem_inc(mask_made, MASK_CREDIT)
            v.sem_inc(t_made, TS)
            v.memset(zeros[:, :], 0.0).then_inc(zeros_ready, 1)
            v.memset(small[:, 8:9], -1.0).then_inc(zeros_ready, 1)
            v.wait_ge(ident_ready, 4)
            DS = 5
            with v.Fori(0, NI) as i:
                for u in range(RING):
                    b = i * RING + u
                    v.wait_ge(row_loaded[u % 2], i * 32 + 16 * (u // 2 + 1))
                    v.tensor_reduce(part[:, :], rowbuf[:, u % 2, :].rearrange("p (a n) -> p a n", a=8), AX_X, ALU.add)\
                        .then_inc(rowsum_done, 1)
                    v.wait_ge(rowsum_done, b + (1 + ROW_CREDIT))
                    v.tensor_reduce(small[:, 0:1], part[:, :], AX_X, ALU.add).then_inc(deg_step, 1)
                    v.wait_ge(deg_step, b * DS + 1)
                    v.tensor_scalar(small[:, 1:2], small[:, 0:1], 1.0, TINY, ALU.add, ALU.max).then_inc(deg_ready, 1)
                    v.tensor_scalar(small[:, 2:3], small[:, 0:1], 1.0, 0.0, ALU.add, ALU.is_gt).then_inc(deg_step, 1)
                    v.wait_ge(deg_step, b * DS + 2)
                    v.wait_ge(pow_ready, b + 1)
                    d = d_all[:, bass.ds(b, 1)]
                    v.tensor_tensor(small[:, 4:5], small[:, 3:4], small[:, 2:3], ALU.mult).then_inc(deg_step, 1)
                    v.wait_ge(deg_step, b * DS + 3)
                    v.tensor_copy(d, small[:, 4:5]).then_inc(deg_step, 1)
                    v.tensor_tensor(small[:, 5:6], small[:, 4:5], small[:, 1:2], ALU.mult).then_inc(deg_step, 1)
                    v.wait_ge(deg_step, b * DS + 5)
                    v.wait_ge(pe_block, b + 1)
                    v.wait_ge(xw_ready, NG)
                    v.tensor_scalar(stat[:, u, :], block_of(xw_g, b), small[:, 4:5], None, ALU.mult)
                    v.tensor_scalar(diag[:, u, :], ident[:, :], small[:, 5:6], None, ALU.mult).then_inc(stat_ready, 1)
            step(v.tensor_tensor(d2_all[:, :], d_all[:, :], d_all[:, :], ALU.mult))
            v.wait_ge(consts, ALL_CONSTS)
            step(v.tensor_tensor(vec[:, 4:5], vec[:, 1:2], vec[:, 0:1], ALU.subtract))
            step(v.tensor_scalar(vec[:, 4:5], vec[:, 4:5], 1.0 / C, None, ALU.mult))
            v.tensor_scalar(turn[:, :], ident[:, :], vec[:, 0:1], vec[:, 4:5], ALU.mult, ALU.add).then_inc(turn_ready, 1)
            for k in range(NG):
                v.wait_ge(hw_done, k + 1)
                v.tensor_tensor(xw_g[:, group(k), :], ps[:, k, :].rearrange("p (b c) -> p b c", c=C),
                                bcast(d2_all[:, group(k)], C), ALU.mult).then_inc(g_ready, 1)
            v.wait_ge(weights_read, 2)
            for head in range(K):
                v.tensor_copy(was[:, head, :], wa[:, 2 * head:2 * head + 1].broadcast_to([P, P])).then_inc(was_ready, 1)
            with v.Fori(0, NI) as i:
                for u in range(RING):
                    b = i * RING + u
                    v.wait_ge(col_loaded[u], i * 16 + 16 * (NI + 1))
                    v.wait_ge(mask_stored[u % SN], i * 32 + 16 * (u // SN + 1))
                    v.tensor_scalar(mtile[:, u % SN, :], colbuf[:, u, :], 0.0, None, ALU.is_gt)\
                        .then_inc(tile_step, 1)
                    v.wait_ge(tile_step, b + 1)
                    own = mtile[:, u % SN, bass.ds(b * P, P)]
                    v.tensor_tensor(own, own, ident_u8[:, :], ALU.max).then_inc(mask_made, 1)

            def stats(z, k, source):
                v.wait_ge(rows_ready[z], k + 1)
                for b in range(k * BPG, (k + 1) * BPG):
                    last = v.bn_stats(bn[:, z // LAST, b, :], source(b))
                last.then_inc(stats_ready[z], 1)

            def moments(z, k):
                v.wait_ge(stats_ready[z], k + 1)
                for b in range(k * BPG, (k + 1) * BPG):
                    last = v.bn_aggr(mv[:, z // LAST, b, :], bn[:, z // LAST, b, :])
                last.then_inc(moments_ready[z], 1)

            def apply(z, k, rows, scale):
                v.wait_ge(scale_ready[z], k + 1)
                for b in range(k * BPG, (k + 1) * BPG):
                    last = v.tensor_scalar(rows[:, b, :], rows[:, b, :], mv[:, z // LAST, b, 0:1], scale[:, b:b + 1],
                                           ALU.subtract, ALU.mult)
                return last

            v.wait_ge(xb2_ready, 1)
            for i in range(NG + 3):
                k = i
                if k < NG:
                    v.wait_ge(tr_done, k + 1)
                    for b in range(k * BPG, (k + 1) * BPG):
                        last = v.scalar_tensor_tensor(out=x1[:, b, :], in0=ps[:, k, cols(b % BPG)],
                                                      scalar=d_all[:, b:b + 1], in1=x1[:, b, :],
                                                      op0=ALU.mult, op1=ALU.add)
                    last.then_inc(rows_ready[0], 1)
                if 0 <= i - STATS < NG:
                    stats(0, i - STATS, lambda b: x1[:, b, :])
                if 0 <= i - MOMENTS < NG:
                    moments(0, i - MOMENTS)
                if 0 <= i - SHIFT < NG:
                    apply(0, i - SHIFT, x1, rstd).then_inc(x1_ready, 1)

            v.wait_ge(st_ready, NG)
            for head in range(K):
                v.tensor_reduce(span[:, head:head + 1], st[:, :, 2 * head + 1], AX_X, ALU.max)
                last = v.tensor_reduce(span[:, K + head:K + head + 1], st[:, :, 2 * head + 1], AX_X, ALU.min)
            step(last)
            v.tensor_scalar(span[:, K:2 * K], span[:, K:2 * K], -1.0, None, ALU.mult).then_inc(span_ready, 1)
            v.wait_ge(top_ready, 1)
            step(v.tensor_tensor(npass_f[:, :], top[:, 0:K], top[:, K:2 * K], ALU.add))
            step(v.tensor_reduce(small[:, 6:7], npass_f[:, :], AX_X, ALU.max))
            step(v.tensor_scalar(small[:, 7:8], small[:, 6:7], 1.0 / WINDOW, 1.1, ALU.mult, ALU.add))
            v.tensor_copy(npass[:, :], small[:, 7:8]).then_inc(npass_ready, 1)

            def head_end(head):
                z = 1 + head
                v.wait_ge(den_step, n * (3 * (head + 1) * NG))
                for i in range(NG + END):
                    k = i
                    if k < NG:
                        v.wait_ge(att_h_done, head * NG + k + 1)
                        for b in range(k * BPG, (k + 1) * BPG):
                            last = v.scalar_tensor_tensor(out=Yw[:, b, :], in0=ps[:, k % 4, cols(b % BPG)],
                                                          scalar=inv_den[:, b:b + 1], in1=x1[:, b, :],
                                                          op0=ALU.mult, op1=ALU.add)
                        last.then_inc(rows_ready[z], 1)
                    if 0 <= i - STATS < NG:
                        stats(z, i - STATS, lambda b: Yw[:, b, :])
                    if 0 <= i - MOMENTS < NG:
                        moments(z, i - MOMENTS)
                    k = i - SHIFT
                    if 0 <= k < NG:
                        v.wait_ge(scale_ready[z], k + 1)
                        v.scalar_tensor_tensor(out=shift[:, group(k)], in0=mv[:, 0, group(k), 0], scalar=-1.0,
                                               in1=rstd[:, group(k)], op0=ALU.mult, op1=ALU.mult)\
                            .then_inc(shift_ready, 1)
                    k = i - ELU
                    if 0 <= k < NG:
                        e = tbuf[:, 2 + k % SN, :]
                        v.wait_ge(y_read, 2 * (head * NG + k) + 2)
                        step(v.tensor_scalar(e, e, 1.0, 1.0 / K, ALU.min, ALU.mult))
                        v.scalar_tensor_tensor(out=e, in0=e, scalar=-1.0 / K, in1=tbuf[:, 4 + k % SN, :],
                                               op0=ALU.add, op1=ALU.add).then_inc(elu_ready, 1)
                    if head == K - 1:
                        k = i - ELU - 1
                        if 0 <= k < NG:
                            v.wait_ge(acc_added, head * NG + k + 1)
                            for b in range(k * BPG, (k + 1) * BPG):
                                last = v.bn_stats(bn[:, 1, b, :], acc[:, b, :])
                            last.then_inc(stats_ready[LAST], 1)
                        if 0 <= k - 1 < NG:
                            moments(LAST, k - 1)
                        if 0 <= k - 2 < NG:
                            apply(LAST, k - 2, acc, r2).then_inc(out_ready, 1)

            n = passes(v)
            v.wait_ge(srow_ready, NG)
            for head in range(K):
                step(v.tensor_copy(gref[:, 0:1], top[:, head:head + 1]))
                if head:
                    v.wait_ge(srow_ready, K * NG)
                    v.wait_ge(att_t_done, head * NG)
                with v.Fori(n * head, n * (head + 1)) as q:
                    done = [0]

                    def pstep(instruction):
                        done[0] += 1
                        instruction.then_inc(pass_step, 1)
                        v.wait_ge(pass_step, q * PASS_STEPS + done[0])

                    v.wait_ge(relu_made, q * GC + 1)
                    v.wait_ge(chunk_done, q * GC + TS)
                    v.wait_ge(den_read, q * NG + NG)
                    s_dst = st[:, :, 2 * head + 1]
                    pstep(v.tensor_scalar(gref[:, 1:2], gref[:, 0:1], -WINDOW, None, ALU.add))
                    v.tensor_scalar(below[:, :], s_dst, gref[:, 0:1], 0.0, ALU.subtract, ALU.min).then_inc(below_ready, 1)
                    pstep(v.tensor_scalar(inside[:, :], s_dst, gref[:, 0:1], None, ALU.is_le))
                    pstep(v.scalar_tensor_tensor(out=inside[:, :], in0=s_dst, scalar=gref[:, 1:2], in1=inside[:, :],
                                                 op0=ALU.is_gt, op1=ALU.mult))

                    def clamp_row(k):
                        v.tensor_scalar(Rrow[:, cols(k, GW)], srow[:, head, cols(k, GW)], gref[:, 0:1], WINDOW,
                                        ALU.add, ALU.min).then_inc(rows_clamped, 1)

                    def weigh(c):
                        for b in range(c * JC, (c + 1) * JC):
                            last = v.tensor_scalar(Yw[:, b, :], x1[:, b, :], r2w[:, b:b + 1], weight[:, b:b + 1],
                                                   ALU.mult, ALU.add)
                        last.then_inc(yw_ready, 1)

                    def chunk(g, c):
                        at = q * GC + g * NC + c
                        v.wait_ge(mask_loaded[c % TS], (q * NG + g) * (16 * USES[c % TS]) + 16 * (c // TS + 1))
                        v.wait_ge(relu_made, at + 2)
                        tile = T[:, c % TS, :, :].rearrange("p b n -> p (b n)")
                        v.scalar_tensor_tensor(out=tile, in0=tile, scalar=1.0,
                                               in1=mring[:, c % TS, :, :].rearrange("p b n -> p (b n)"),
                                               op0=ALU.add, op1=ALU.mult).then_inc(t_made, 1)

                    def row_scale(g, stage):
                        at = (q * NG + g) * ROW_STEPS
                        s_src, own_ref = srow[:, head, bass.ds(g * GW, GW)], row_of(ref, g)
                        if stage == 0:
                            v.tensor_scalar(log_scale[:, :], s_src, gref[:, 0:1], None, ALU.add)
                            v.tensor_scalar(above[:, :], s_src, gref[:, 0:1], WINDOW, ALU.add, ALU.min)\
                                .then_inc(row_step, 1)
                        elif stage == 1:
                            v.wait_ge(row_step, at + 1)
                            v.scalar_tensor_tensor(out=log_scale[:, :], in0=above[:, :], scalar=SLOPE - 1.0,
                                                   in1=log_scale[:, :], op0=ALU.mult, op1=ALU.add).then_inc(row_step, 1)
                        elif stage == 2:
                            v.wait_ge(sums_zeroed, 2 * head + 3)
                            v.wait_ge(row_step, at + 2)
                            v.tensor_tensor(above[:, :], own_ref, log_scale[:, :], ALU.subtract).then_inc(row_step, 1)
                        else:
                            v.wait_ge(row_step, at + 3)
                            v.scalar_tensor_tensor(out=above[:, :], in0=row_of(den, g), scalar=0.0, in1=above[:, :],
                                                   op0=ALU.is_gt, op1=ALU.mult).then_inc(row_step, 1)
                            v.wait_ge(row_step, at + 4)
                            v.tensor_tensor(own_ref, log_scale[:, :], above[:, :], ALU.add).then_inc(row_step, 1)

                    def add_sums(g):
                        v.wait_ge(chunk_done, (q * NG + g) * NC + (NC + TS))
                        v.wait_ge(scale_row_ready, q * NG + (g + 1))
                        v.tensor_tensor(scaled[:, :], bank(g), scale_row[:, :], ALU.mult).then_inc(sum_step, 1)
                        v.wait_ge(sum_step, q * NG + (g + 1))
                        v.tensor_tensor(row_of(num, g), row_of(num, g), scaled[:, :], ALU.add).then_inc(num_ready, 1)

                    def invert_den(g):
                        at = (q * NG + g) * 3
                        v.wait_ge(den_read, q * NG + (g + (1 + NG)))
                        v.tensor_tensor(scaled[:, :].rearrange("p (b n) -> p b n", n=P),
                                        row_of(den, g).rearrange("p (b n) -> p b n", n=P),
                                        ident[:, :].unsqueeze(1).broadcast_to([P, BPG, P]), ALU.mult).then_inc(den_step, 1)
                        v.wait_ge(den_step, at + 1)
                        v.tensor_reduce(node_den[:, :], scaled[:, :].rearrange("p (b n) -> p b n", n=P), AX_X, ALU.add)\
                            .then_inc(den_step, 1)
                        v.wait_ge(den_step, at + 2)
                        v.reciprocal(inv_den[:, bass.ds(g * BPG, BPG)], node_den[:, :]).then_inc(den_step, 1)

                    clamp_row(0)
                    v.wait_ge(exp_ready, q + 1)
                    pstep(v.tensor_tensor(weight[:, :], weight[:, :], inside[:, :], ALU.mult))
                    pstep(v.tensor_tensor(r2w[:, :], weight[:, :], r2[:, :], ALU.mult))
                    assert done[0] == PASS_STEPS
                    weigh(0)
                    for c in range(NC):
                        if c + 1 < NC:
                            clamp_row(c + 1)
                        chunk(0, c)
                        if c + 1 < NC:
                            weigh(c + 1)
                        for stage in range(4):
                            if c == max(NC - 4 + stage, 0):
                                row_scale(0, stage)
                    with v.Fori(1, NG) as g:
                        for c in range(NC):
                            chunk(g, c)
                            if c == NC // 2 - 1:
                                add_sums(g - 1)
                            if c == NC - 1:
                                invert_den(g - 1)
                            for stage in range(4):
                                if c == max(NC - 4 + stage, 0):
                                    row_scale(g, stage)
                    add_sums(NG - 1)
                    invert_den(NG - 1)
                    v.tensor_copy(gref[:, 0:1], gref[:, 1:2]).then_inc(gref_moved, 1)
                    v.wait_ge(gref_moved, q + 1)
                head_end(head)

        @block.tensor
        def _(pe):
            def multiply(*args, **kw):
                return pe.matmul(*args, skip_group_check=True, **kw)

            def zero_banks(start, stop, k):
                return multiply(ps[:, k, :], zeros[:, 0:P], zeros[:, :], start=start, stop=stop)

            def aggregate_last(extra):
                u = RING - 1
                own = ps[:, NG - 1, cols(u)]
                multiply(own, stat[:, u, :], ident[:, :], start=False, stop=False)
                if extra:
                    multiply(own, b1bc[:, :], diag[:, u, :], start=False, stop=False)
                for k in range(NG):
                    last = multiply(ps[:, k, :], stat[:, u, :], colbuf[:, u, cols(k, GW)], start=False, stop=k < NG - 1)
                    last.then_inc(agg_done if k < NG - 1 else pe_block, 1)
                multiply(ps[:, NG - 1, 0:2], zeros[:, 0:P], zeros[:, 0:2], start=False, stop=True).then_inc(agg_done, 1)

            def aggregate(i, u, extra):
                for k in range(NG):
                    multiply(ps[:, k, :], stat[:, u, :], colbuf[:, u, cols(k, GW)], start=False, stop=False)
                own = ps[:, bass.ds(i, 1), cols(u)].rearrange("p o n -> p (o n)")
                last = multiply(own, stat[:, u, :], ident[:, :], start=False, stop=False)
                if extra:
                    last = multiply(own, b1bc[:, :], diag[:, u, :], start=False, stop=False)
                last.then_inc(pe_block, 1)

            def spread_source(head, k, at):
                if k == 0:
                    pe.wait_ge(was_ready, head + 1)
                multiply(ps[:, at, :], was[:, head, :], xnT[:, cols(k, GW)], start=True, stop=True).then_inc(s_done, 1)

            pe.sem_inc(pe_block, COL_CREDIT)
            pe.sem_inc(chunk_done, TS)
            pe.wait_ge(first_loaded, ALL_FIRST)
            for k in range(NG):
                pe.wait_ge(xT_loaded[k], 16)
                for b in range(k * BPG, (k + 1) * BPG):
                    last = multiply(ps[:, k, cols(b % BPG)], xnT[:, cols(b)], w1[:, :], start=True, stop=True)
                last.then_inc(xw_done, 1)
            pe.wait_ge(zeros_ready, 2)
            for k in range(NG):
                pe.wait_ge(xw_ready, k + 1)
                zero_banks(True, False, k)
            with pe.Fori(0, NI - 1) as i:
                for u in range(RING):
                    pe.wait_ge(col_loaded[u], i * 16 + 16)
                    pe.wait_ge(stat_ready, i * RING + (u + 1))
                    aggregate(i, u, True)
            for u in range(RING):
                pe.wait_ge(col_loaded[u], NI * 16)
                pe.wait_ge(stat_ready, (NI - 1) * RING + (u + 1))
                if u < RING - 1:
                    aggregate(NI - 1, u, True)
            aggregate_last(True)
            pe.wait_ge(consts, ALL_CONSTS)
            for k in range(NG):
                pe.wait_ge(hT_ready, k + 1)
                for ib in range(BPG):
                    last = multiply(ps[:, k, cols(ib)], hT[:, k % SN, cols(ib)], w2[:, :], start=True, stop=True)
                last.then_inc(hw_done, 1)
            pe.wait_ge(g_ready, 1)
            pe.wait_ge(turn_ready, 1)
            for head in range(K):
                multiply(ps[:, 0, cols(head)], turn[:, :], ff0T[:, head, :], start=True, stop=True)
            for head in range(K):
                last = multiply(ps[:, 0, K * C + 2 * head:K * C + 2 * head + 2], ff0[:, head, :], attnT[:, head, :],
                                start=True, stop=True)
            last.then_inc(weights_done, 1)
            for k in list(range(1, NG)) + [0]:
                pe.wait_ge(g_ready, k + 1)
                if k == 0:
                    pe.wait_ge(weights_read, 2)
                zero_banks(True, False, k)
            with pe.Fori(0, NI - 1) as i:
                for u in range(RING):
                    pe.wait_ge(col_loaded[u], i * 16 + 16 * (NI + 1))
                    pe.wait_ge(g_copied, i * RING + (u + 1))
                    aggregate(i, u, False)
            for u in range(RING):
                pe.wait_ge(col_loaded[u], 2 * NI * 16)
                pe.wait_ge(g_copied, (NI - 1) * RING + (u + 1))
                if u < RING - LATE:
                    aggregate(NI - 1, u, False)
            for u in range(RING - LATE, RING):
                multiply(ps[:, NG - 1, cols(u)], stat[:, u, :], ident[:, :], start=False, stop=False)
            for i in range(NG + TURN + 4):
                k = i
                if k < NG:
                    for u in range(RING - LATE, RING):
                        last = multiply(ps[:, k, :], stat[:, u, :], colbuf[:, u, cols(k, GW)],
                                        start=False, stop=u == RING - 1)
                    last.then_inc(agg_done, 1)
                k = i - 1
                if 0 <= k < NG:
                    pe.wait_ge(accT_ready, k + 1)
                    for ib in range(BPG):
                        last = pe.transpose(ps[:, k, cols(ib)], hT[:, k % SN, cols(ib)], ident[:, :])
                    last.then_inc(tr_done, 1)
                k = i - TURN - 1
                if 0 <= k < NG:
                    pe.wait_ge(xn_ready, (k + 1) * BPG)
                    for ib in range(BPG):
                        last = pe.transpose(ps[:, k, cols(ib)], Yw[:, k * BPG + ib, :], ident[:, :])
                    last.then_inc(xnt_done, 1)
                k = i - TURN - 2
                if 0 <= k < NG:
                    pe.wait_ge(xnT_ready, k + 1)
                    for ib in range(BPG):
                        last = multiply(ps[:, k, cols(ib, 2 * K)], xnT[:, cols(k * BPG + ib)], wa[:, :],
                                        start=True, stop=True)
                    last.then_inc(st_done, 1)
                k = i - TURN - 3
                if 0 <= k < NG:
                    pe.wait_ge(st_ready, k + 1)
                    spread_source(0, k, k)
            pe.wait_ge(srow_ready, NG)
            pe.wait_ge(mean_ready, 1)
            n = passes(pe)
            for head in range(K):
                with pe.Fori(n * head, n * (head + 1)) as q:
                    def chunk(g, c):
                        at = q * GC + g * NC + c
                        pe.wait_ge(t_made, at + (TS + 1))
                        if c == 0:
                            pe.wait_ge(den_read, q * NG + (g + 1))
                        for j in range(JC):
                            last = multiply(bank(g), Yw[:, c * JC + j, :], T[:, c % TS, j, :],
                                            start=c == 0 and j == 0, stop=c == NC - 1 and j == JC - 1)
                        last.then_inc(chunk_done, 1)

                    def spread_den(g):
                        pe.wait_ge(num_ready, q * NG + (g + 1))
                        multiply(bank(g), mean[:, :], row_of(num, g), start=True, stop=True).then_inc(den_done, 1)

                    for c in range(NC):
                        pe.wait_ge(yw_ready, q * NC + (c + 1))
                        chunk(0, c)
                    with pe.Fori(1, NG) as g:
                        for c in range(NC):
                            chunk(g, c)
                            if c == NC // 2 - 1:
                                spread_den(g - 1)
                    spread_den(NG - 1)
                for i in range(NG + SHIFT + 2):
                    k = i
                    if k < NG:
                        if k == 0:
                            pe.wait_ge(den_read, n * ((head + 1) * NG) + (NG - 1))
                        if k == min(4, NG - 1):
                            pe.wait_ge(den_read, n * ((head + 1) * NG) + NG)
                        if k >= 4:
                            pe.wait_ge(rows_ready[1 + head], k - 3)
                            if head + 1 < K:
                                pe.wait_ge(srow_ready, (head + 1) * NG + k - 3)
                        for ib in range(BPG):
                            last = multiply(ps[:, k % 4, cols(ib)], num[:, cols(k * BPG + ib)], fold[:, head, :],
                                            start=True, stop=True)
                        last.then_inc(att_h_done, 1)
                    k = i - STATS - 1
                    if 0 <= k < NG and head + 1 < K:
                        pe.wait_ge(rows_ready[1 + head], k + 1)
                        spread_source(head + 1, k, k % 4)
                    k = i - SHIFT - 1
                    if 0 <= k < NG:
                        m = head * NG + k
                        pe.wait_ge(att_ready, (m + 1) * BPG)
                        if k >= SN:
                            pe.wait_ge(att_t_ready, m - 1)
                        for ib in range(BPG):
                            last = pe.transpose(ps[:, 4 + k % SN, cols(ib)], Yw[:, k * BPG + ib, :], ident[:, :])
                        last.then_inc(att_t_done, 1)
                    k = i - SHIFT - 2
                    if 0 <= k < NG:
                        m = head * NG + k
                        pe.wait_ge(att_t_ready, m + 1)
                        if k >= SN:
                            pe.wait_ge(y_read, 2 * (m - 1))
                        for ib in range(BPG):
                            last = multiply(ps[:, 6 + k % SN, cols(ib)], tbuf[:, k % SN, cols(ib)],
                                            ff1T[:, head, :], start=True, stop=True)
                        last.then_inc(y_done, 1)
                if head + 1 < K:
                    pe.wait_ge(srow_ready, (head + 2) * NG)
                    pe.wait_ge(y_read, 2 * (head + 1) * NG)


_INS = ["x", "xT", "adj", "adjT", "W1", "b1", "W2", "b2", "ff0", "ff0T", "ff1T", "attnT",
        "ln1_g", "ln1_b", "ln2_g", "ln2_b"]


def kernel(x, adj, L0_gnn_W1, L0_gnn_b1, L0_gnn_W2, L0_gnn_b2, L1_gnn_ff0_w, L1_gnn_ff1_w, L1_gnn_attn_w,
           L1_gnn_g1, L1_gnn_b1, L1_gnn_g2, L1_gnn_b2):
    import numpy as np
    from concourse import bacc
    from concourse.bass_utils import run_bass_kernel_spmd

    ff0, ff1, attn = np.asarray(L1_gnn_ff0_w), np.asarray(L1_gnn_ff1_w), np.asarray(L1_gnn_attn_w)
    heads, c = ff0.shape[0], ff0.shape[1]
    given = {
        "x": x, "xT": np.asarray(x).T, "adj": adj, "adjT": np.asarray(adj).T,
        "W1": L0_gnn_W1, "b1": L0_gnn_b1, "W2": L0_gnn_W2, "b2": L0_gnn_b2,
        "ff0": ff0, "ff0T": ff0.transpose(0, 2, 1), "ff1T": ff1.transpose(0, 2, 1),
        "attnT": attn.reshape(heads, 2, c).transpose(2, 0, 1),
        "ln1_g": L1_gnn_g1, "ln1_b": L1_gnn_b1, "ln2_g": L1_gnn_g2, "ln2_b": L1_gnn_b2,
    }
    arrays = {name: np.ascontiguousarray(given[name]) for name in _INS}
    nc = bacc.Bacc("TRN2", target_bir_lowering=False, num_devices=1)
    t = {name: nc.dram_tensor(f"in_{name}", arrays[name].shape, F32, kind="ExternalInput").ap() for name in _INS}
    out = nc.dram_tensor("out", arrays["x"].shape, F32, kind="ExternalOutput").ap()
    build(nc, t, out)
    r = run_bass_kernel_spmd(nc, [{f"in_{name}": a for name, a in arrays.items()}], core_ids=[0])
    return r.results[0]["out"]
```

```python
from contextlib import ExitStack

import concourse.bass as bass
from concourse import mybir

F32 = mybir.dt.float32
BF16 = mybir.dt.bfloat16
U8 = mybir.dt.uint8
I32 = mybir.dt.int32
ALU = mybir.AluOpType
ACT = mybir.ActivationFunctionType
AX_X = mybir.AxisListType.X

P = 128
GW = 512
BPG = GW // P
JC = 4
RING = 4
SLOPE = 0.01
WINDOW = 48.0
LN_EPS = 1e-5
TINY = 1e-30


def bcast(column, n):
    return column.unsqueeze(2).broadcast_to([column.shape[0], column.shape[1], n])


def build(nc, t, out):
    N, C = t["x"].shape
    K = t["ff0"].shape[0]
    B = N // P
    NG = N // GW
    NC = B // JC
    NI = B // RING
    SN = 2
    TS = min(4, NC)
    assert C == P and K == 2 and RING == BPG and NI > 3 and NG <= 8 and NC == NG

    mask_dram = nc.dram_tensor("mask", [B, P, N], U8).ap()

    ctx = ExitStack()
    with ctx:
        block_scope = ctx

        def sb(name, shape, dtype, scope=None):
            return (scope or block_scope).enter_context(nc.sbuf_tensor(name, shape, dtype))

        def sem(name):
            return block_scope.enter_context(nc.semaphore(name))

        x1 = sb("x1", [P, B, C], F32)
        xnT_acc = sb("xnT_acc", [P, B, C], F32)
        ident = sb("ident", [P, P], F32)
        ident_u8 = sb("ident_u8", [P, P], U8)
        zeros = sb("zeros", [P, GW], BF16)
        mean = sb("mean", [P, P], F32)
        w1 = sb("w1", [P, C], F32)
        w2 = sb("w2", [P, C], F32)
        b1bc = sb("b1bc", [P, C], F32)
        b2bc = sb("b2bc", [P, C], F32)
        vec = sb("vec", [P, 5], F32)
        ff0 = sb("ff0", [P, K, C], F32)
        ff0T = sb("ff0T", [P, K, C], F32)
        gain_mix = sb("gain_mix", [P, P], F32)
        fold = sb("fold", [P, K, C], F32)
        ff1T = sb("ff1T", [P, K, C], F32)
        attnT = sb("attnT", [P, K, 2], F32)
        wa = sb("wa", [P, K * 2], F32)
        was = sb("was", [P, K, P], F32)
        half = sb("half", [P, B], F32)
        d_all = sb("d_all", [P, B], F32)
        d2_all = sb("d2_all", [P, B], F32)
        small = sb("small", [P, 16], F32)
        bn = sb("bn", [P, 2, B, 6], F32)
        mv = sb("mv", [P, 2, B, 2], F32)
        rstd = sb("rstd", [P, B], F32)
        r2 = sb("r2", [P, B], F32)
        shift = sb("shift", [P, B], F32)
        st = sb("st", [P, B, K * 2], F32)
        span = sb("span", [P, 2 * K], F32)
        top = sb("top", [P, 2 * K], F32)
        npass_f = sb("npass_f", [P, 2], F32)
        npass = sb("npass", [P, 1], I32)
        gref = sb("gref", [P, 2], F32)
        below = sb("below", [P, B], F32)
        inside = sb("inside", [P, B], F32)
        ratio = sb("ratio", [P, B], F32)
        weight = sb("weight", [P, B], F32)
        inv_den = sb("inv_den", [P, B], F32)
        node_den = sb("node_den", [P, BPG], F32)
        r2w = sb("r2w", [P, B], F32)

        first = ExitStack()
        rowbuf = sb("rowbuf", [P, 2, N], F32, first)
        colbuf = sb("colbuf", [P, RING, N], F32, first)
        xw_g = sb("xw_g", [P, B, C], F32, first)
        mtile = sb("mtile", [P, 2, N], U8, first)
        stat = sb("stat", [P, RING, C], F32, first)
        diag = sb("diag", [P, RING, C], F32, first)
        hT = sb("hT", [P, 2, GW], F32, first)
        part = sb("part", [P, 8], F32, first)
        first.close()

        Yw = sb("Yw", [P, B, C], F32)
        srow = sb("srow", [P, K, N], F32)
        Rrow = sb("Rrow", [P, N], F32)
        ref = sb("ref", [P, N], F32)
        den = sb("den", [P, N], F32)
        num = sb("num", [P, N], F32)
        T = sb("T", [P, TS, JC, GW], F32)
        mring = sb("mring", [P, TS, JC, GW], U8)
        log_scale = sb("log_scale", [P, GW], F32)
        above = sb("above", [P, GW], F32)
        scale_row = sb("scale_row", [P, GW], F32)
        scaled = sb("scaled", [P, GW], F32)
        tbuf = T[:, :, :, :].rearrange("p a b c -> p (a b) c")

        ps = ctx.enter_context(nc.psum_tensor("ps", [P, 8, GW], F32))

        def sems(names):
            return [sem(name) for name in names.split()]

        x_loaded = [sem(f"x_loaded{k}") for k in range(NG)]
        first_loaded, consts, xT_done, xT_ready, ident_ready, zeros_ready, skip_ready = sems(
            "first_loaded consts xT_done xT_ready ident_ready zeros_ready skip_ready")
        row_loaded = sems("row_loaded0 row_loaded1")
        col_loaded = [sem(f"col_loaded{s}") for s in range(RING)]
        mask_stored = sems("mask_stored0 mask_stored1")
        mask_loaded = [sem(f"mask_loaded{s}") for s in range(TS)]
        xw_done, xw_ready, rowsum_done, deg_step, deg_ready, pow_ready = sems(
            "xw_done xw_ready rowsum_done deg_step deg_ready pow_ready")
        stat_ready, pe_block, agg_done, hT_ready, hw_done, g_ready, g_copied, mask_made, tile_step = sems(
            "stat_ready pe_block agg_done hT_ready hw_done g_ready g_copied mask_made tile_step")
        dve_step, accT_ready, tr_done, xn_ready, xnt_done, xnT_ready = sems(
            "dve_step accT_ready tr_done xn_ready xnt_done xnT_ready")
        weights_done, weights_read, st_done, st_ready, span_ready, top_ready, npass_ready, was_ready = sems(
            "weights_done weights_read st_done st_ready span_ready top_ready npass_ready was_ready")
        s_done, srow_ready, sums_zeroed, pass_step, below_ready, exp_ready, rows_clamped, R_ready, yw_ready = sems(
            "s_done srow_ready sums_zeroed pass_step below_ready exp_ready rows_clamped R_ready yw_ready")
        relu_made, t_made, chunk_done, row_step, scale_row_ready, sum_step, num_ready, den_done, den_read = sems(
            "relu_made t_made chunk_done row_step scale_row_ready sum_step num_ready den_done den_read")
        mean_ready, gain_mix_ready, den_step, att_h_done, att_ready, att_t_done, att_t_ready, y_done, exp_y_ready = sems(
            "mean_ready gain_mix_ready den_step att_h_done att_ready att_t_done att_t_ready y_done exp_y_ready")
        out_ready, stored, loads_started, gref_moved, relus_started = sems("out_ready stored loads_started gref_moved relus_started")

        LAST = K + 1
        rows_ready, stats_ready, moments_ready, scale_ready, shift_ready = (
            [sem(f"{what}{z}") for z in range(K + 2)]
            for what in ("rows_ready", "stats_ready", "moments_ready", "scale_ready", "shift_ready"))
        x1_ready, r2_ready, elu_ready, acc_added, pool_step = sems("x1_ready r2_ready elu_ready acc_added pool_step")

        adj_rows = t["adj"].rearrange("(b p) n -> b p n", p=P)
        adj_cols = t["adjT"].rearrange("(b p) n -> b p n", p=P)
        out_v = out.rearrange("(b p) c -> p b c", p=P)
        xnT = xnT_acc[:, :, :].rearrange("p b c -> p (b c)")
        acc = xnT_acc

        def block_of(tensor, b):
            return tensor[:, bass.ds(b, 1), :].rearrange("p o n -> p (o n)")

        def row_of(tensor, g):
            return tensor[:, bass.ds(g * GW, GW)]

        def bank(g):
            return ps[:, bass.ds(g, 1), :].rearrange("p o n -> p (o n)")

        def dram_block(tensor, b):
            return tensor[bass.ds(b, 1), :, :].rearrange("o p n -> (o p) n")

        def group(k):
            return slice(k * BPG, (k + 1) * BPG)

        def cols(k, n=P):
            return slice(k * n, (k + 1) * n)

        FIRST = [(w1[:, :], t["W1"]), (b1bc[:, :], t["b1"].partition_broadcast(P))]
        CONSTS = [
            (w2[:, :], t["W2"]), (b2bc[:, :], t["b2"].partition_broadcast(P)),
            (ff0[:, :, :], t["ff0"].rearrange("k o i -> o k i")),
            (ff0T[:, :, :], t["ff0T"].rearrange("k i o -> i k o")),
            (ff1T[:, :, :], t["ff1T"].rearrange("k i o -> i k o")),
            (attnT[:, :, :], t["attnT"]),
        ] + [(vec[:, m:m + 1], t[name].rearrange("(p o) -> p o", o=1))
             for m, name in enumerate(("ln1_g", "ln1_b", "ln2_g", "ln2_b"))]
        ALL_CONSTS = 16 * len(CONSTS)
        ALL_FIRST = 16 * len(FIRST)

        ROW_CREDIT, COL_CREDIT = 2, RING
        STORE_CREDIT = 16
        MASK_CREDIT = B + COL_CREDIT
        AHEAD = LATE = 2
        ROUNDS = NI - 2
        FIRST_TURNS = [(u, B - RING + u) for u in range(RING)] + [(u, u) for u in range(AHEAD)]
        GC = NG * NC
        PASS_STEPS = 5
        ROW_STEPS = 5
        USES = [sum(c % TS == s for c in range(NC)) for s in range(TS)]
        MAX_PASSES = 1 << 12
        STATS, MOMENTS, SHIFT = 1, 2, 3
        TURN = SHIFT + 1
        ELU = 7
        ES = 4
        END = ELU + 1 + 1 + 1

        def passes(eng):
            eng.wait_ge(npass_ready, 1)
            return eng.value_load(npass[0:1, 0:1], min_val=1, max_val=MAX_PASSES)

        block = ctx.enter_context(nc.Block())

        @block.sync
        def _(sp):
            sp.wait_ge(x_loaded[NG // 2], 16)
            with sp.Fori(0, NI) as i:
                for u in range(RING):
                    b = i * RING + u
                    sp.wait_ge(rowsum_done, b + 1)
                    sp.dma_start(rowbuf[:, u % 2, :], dram_block(adj_rows, b)).then_inc(row_loaded[u % 2], 16)
                    sp.wait_ge(pe_block, b + 1)
                    sp.dma_start(colbuf[:, u, :], dram_block(adj_cols, b)).then_inc(col_loaded[u], 16)
            for u in range(AHEAD):
                sp.wait_ge(rowsum_done, B + ROW_CREDIT)
                sp.dma_start(rowbuf[:, u, :], dram_block(adj_cols, u)).then_inc(row_loaded[u], 16)

            def reload(u, b, turn):
                sp.wait_ge(pe_block, turn + (1 + MASK_CREDIT))
                sp.wait_ge(mask_made, turn + (1 + MASK_CREDIT))
                sp.dma_start(colbuf[:, u, :], dram_block(adj_cols, b)).then_inc(col_loaded[u], 16)

            for u in range(RING):
                reload(u, AHEAD + u, u)
            with sp.Fori(1, ROUNDS) as i:
                for u in range(RING):
                    reload(u, i * RING + (AHEAD + u), i * RING + (AHEAD + u))
            for u in range(LATE):
                reload(u, ROUNDS * RING + AHEAD + u, ROUNDS * RING + AHEAD + u)
            for s in range(SN):
                sp.wait_ge(mask_stored[s], 16 * (B // SN) + STORE_CREDIT)
            n = passes(sp)
            with sp.Fori(0, n * K) as q:
                with sp.Fori(0, NG) as g:
                    for c in range(NC):
                        sp.wait_ge(t_made, q * GC + g * NC + (c + 1))
                        sp.sem_inc(loads_started, 1)
                        sp.dma_start(mring[:, c % TS, :, :],
                                     mask_dram[cols(c, JC), :, bass.ds(g * GW, GW)].rearrange("b p n -> p b n"))\
                            .then_inc(mask_loaded[c % TS], 16)
            for k in range(NG):
                sp.wait_ge(out_ready, k + 1)
                sp.dma_start(out_v[:, group(k), :], acc[:, group(k), :]).then_inc(stored, 16)
            sp.wait_ge(stored, 16 * NG)

        @block.gpsimd
        def _(pool):
            pool.memset(ident[:, :], 0.0).then_inc(ident_ready, 1)
            pool.memset(half[:, :], -0.5).then_inc(ident_ready, 1)
            pool.wait_ge(ident_ready, 2)
            pool.affine_select(out=ident[:, :], in_=ident[:, :], compare_op=ALU.not_equal, fill=1.0, base=0,
                               pattern=[[-1, P]], channel_multiplier=1).then_inc(ident_ready, 1)
            pool.wait_ge(ident_ready, 3)
            pool.tensor_copy(ident_u8[:, :], ident[:, :]).then_inc(ident_ready, 1)
            pool.memset(mean[:, :], 1.0 / C).then_inc(mean_ready, 1)
            with pool.Fori(0, B) as b:
                pool.wait_ge(deg_ready, b + 1)
                pool.tensor_tensor(small[:, 3:4], small[:, 1:2], half[:, 0:1], ALU.pow).then_inc(pow_ready, 1)
            pool.wait_ge(consts, ALL_CONSTS)
            pool.wait_ge(g_ready, NG)
            own = xnT_acc[:, :, :]
            pool.tensor_tensor(own, xw_g[:, :, :], bcast(d_all[:, :], C), ALU.mult).then_inc(skip_ready, 1)
            pool.tensor_tensor(x1[:, :, :], x1[:, :, :], b2bc[:, :].unsqueeze(1).broadcast_to([P, B, C]), ALU.add)\
                .then_inc(skip_ready, 1)
            pool.wait_ge(skip_ready, 2)
            pool.tensor_tensor(x1[:, :, :], x1[:, :, :], own, ALU.add).then_inc(skip_ready, 1)
            done = [0]

            def pstep(instruction):
                done[0] += 1
                instruction.then_inc(pool_step, 1)
                pool.wait_ge(pool_step, done[0])

            def norm_scale(z, k, scale):
                pool.wait_ge(moments_ready[z], k + 1)
                pstep(pool.tensor_scalar(scale[:, group(k)], mv[:, z // LAST, group(k), 1], LN_EPS, 1.0, ALU.add, ALU.mult))
                pool.tensor_tensor(scale[:, group(k)], scale[:, group(k)], half[:, group(k)], ALU.pow)\
                    .then_inc(scale_ready[z], 1)

            for k in range(NG):
                norm_scale(0, k, rstd)
                pool.wait_ge(scale_ready[0], k + 1)
                r = r2[:, group(k)]
                pstep(pool.tensor_tensor(r, rstd[:, group(k)], rstd[:, group(k)], ALU.mult))
                pstep(pool.tensor_tensor(r, r, mv[:, 0, group(k), 1], ALU.mult))
                pstep(pool.tensor_scalar(r, r, LN_EPS, 1.0, ALU.add, ALU.mult))
                pool.tensor_tensor(r, r, half[:, group(k)], ALU.pow).then_inc(r2_ready, 1)
            pool.wait_ge(span_ready, 1)
            pool.partition_all_reduce(top[:, :], span[:, :], P, bass.bass_isa.ReduceOp.max).then_inc(top_ready, 1)
            pool.memset(ref[:, :], 0.0).then_inc(sums_zeroed, 1)
            pool.memset(den[:, :], 0.0).then_inc(sums_zeroed, 1)
            pool.memset(num[:, :], 0.0).then_inc(sums_zeroed, 1)
            for head in range(K):
                if head + 1 < K:
                    pool.wait_ge(rows_ready[1 + head], 1)
                    pool.memset(den[:, :], 0.0).then_inc(sums_zeroed, 1)
                for i in range(NG + END):
                    k = i - MOMENTS
                    if 0 <= k < NG:
                        norm_scale(1 + head, k, rstd)
                    k = i - ELU
                    if 0 <= k < NG:
                        m = head * NG + k
                        base = (x1 if head == 0 else acc)[:, group(k), :].rearrange("p b c -> p (b c)")
                        pool.wait_ge(elu_ready, m + 1)
                        pool.tensor_tensor(acc[:, group(k), :].rearrange("p b c -> p (b c)"), base, tbuf[:, ES + k % ES, :],
                                           ALU.add).then_inc(acc_added, 1)
                    k = i - ELU - 1 - 1
                    if 0 <= k < NG and head == K - 1:
                        norm_scale(LAST, k, r2)
                if head + 1 < K:
                    pool.wait_ge(att_h_done, (head + 1) * NG)
                    pool.memset(num[:, :], 0.0).then_inc(sums_zeroed, 1)

        @block.scalar
        def _(act):
            for dst, src in FIRST:
                act.dma_start(dst, src).then_inc(first_loaded, 16)
            for k in range(NG):
                act.dma_start(x1[:, group(k), :], t["x"].rearrange("(b p) c -> p b c", p=P)[:, group(k), :])\
                    .then_inc(x_loaded[k], 16)
            act.sem_inc(relu_made, 1)
            act.sem_inc(den_read, NG)
            for s in range(SN):
                act.sem_inc(mask_stored[s], STORE_CREDIT)
            for i in range(NG + 1):
                k = i
                if k < NG:
                    act.wait_ge(xT_done, k + 1)
                    act.activation(xnT[:, cols(k, GW)], ps[:, k, :], ACT.Copy).then_inc(xT_ready, 1)
                k = i - 1
                if k >= 0:
                    act.wait_ge(xw_done, k + 1)
                    act.activation(xw_g[:, group(k), :].rearrange("p b c -> p (b c)"), ps[:, k, :], ACT.Copy)\
                        .then_inc(xw_ready, 1)
            for dst, src in CONSTS:
                act.dma_start(dst, src).then_inc(consts, 16)
            for k in range(NG):
                act.wait_ge(agg_done, k + 1)
                if k >= SN:
                    act.wait_ge(hw_done, k - 1)
                act.activation(hT[:, k % SN, :], ps[:, k, :], ACT.Relu).then_inc(hT_ready, 1)
            act.wait_ge(weights_done, 1)
            act.activation(fold[:, :, :].rearrange("p k c -> p (k c)"), ps[:, 0, 0:K * C], ACT.Copy)\
                .then_inc(weights_read, 1)
            act.activation(wa[:, :], ps[:, 0, K * C:K * (C + 2)], ACT.Copy).then_inc(weights_read, 1)
            act.wait_ge(g_ready, NG)

            def supply(turn, u, b, tile):
                act.wait_ge(pe_block, turn + (MASK_CREDIT - 1))
                act.activation(stat[:, u, :], block_of(xw_g, b), ACT.Copy).then_inc(g_copied, 1)
                act.wait_ge(mask_made, turn + (1 + MASK_CREDIT))
                act.dma_start(dram_block(mask_dram, b), mtile[:, tile, :]).then_inc(mask_stored[tile], 16)

            for turn, (u, b) in enumerate(FIRST_TURNS):
                supply(turn, u, b, turn % SN)
            with act.Fori(0, ROUNDS) as i:
                for u in range(RING):
                    supply(i * RING + (len(FIRST_TURNS) + u), u, i * RING + (AHEAD + u), u % SN)
            for u in range(LATE):
                supply(B - LATE + u, u, ROUNDS * RING + AHEAD + u, u % SN)

            def source_row(head, k, at):
                act.wait_ge(s_done, head * NG + k + 1)
                act.activation(srow[:, head, cols(k, GW)], ps[:, at, :], ACT.Copy).then_inc(srow_ready, 1)

            for i in range(NG + TURN + 4):
                k = i
                if k < NG:
                    act.wait_ge(agg_done, NG + k + 1)
                    if k >= SN:
                        act.wait_ge(tr_done, k - 1)
                    act.activation(hT[:, k % SN, :], ps[:, k, :], ACT.Copy).then_inc(accT_ready, 1)
                k = i - TURN
                if 0 <= k < NG:
                    act.wait_ge(x1_ready, k + 1)
                    act.wait_ge(r2_ready, k + 1)
                    for b in range(k * BPG, (k + 1) * BPG):
                        act.activation(Yw[:, b, :], x1[:, b, :], ACT.Copy, scale=r2[:, b:b + 1]).then_inc(xn_ready, 1)
                k = i - TURN - 1
                if 0 <= k < NG:
                    act.wait_ge(xnt_done, k + 1)
                    act.activation(xnT[:, cols(k, GW)], ps[:, k, :], ACT.Identity,
                                   scale=vec[:, 0:1], bias=vec[:, 1:2]).then_inc(xnT_ready, 1)
                k = i - TURN - 2
                if 0 <= k < NG:
                    act.wait_ge(st_done, k + 1)
                    act.activation(st[:, group(k), :].rearrange("p b k -> p (b k)"), ps[:, k, 0:BPG * 2 * K], ACT.Copy)\
                        .then_inc(st_ready, 1)
                k = i - TURN - 3
                if 0 <= k < NG:
                    source_row(0, k, k)

            def head_end(head):
                for i in range(NG + (END if head == K - 1 else SHIFT + 3)):
                    k = i - SHIFT - 2
                    if 0 <= k < NG:
                        m = head * NG + k
                        act.wait_ge(att_t_done, m + 1)
                        if k >= ES:
                            act.wait_ge(y_done, m - (ES - 1))
                        act.activation(tbuf[:, k % ES, :], ps[:, 4 + k % SN, :], ACT.Identity,
                                       scale=vec[:, 2:3], bias=vec[:, 3:4]).then_inc(att_t_ready, 1)
                    k = i - SHIFT - 3
                    if 0 <= k < NG:
                        m = head * NG + k
                        act.wait_ge(y_done, m + 1)
                        if k >= ES:
                            act.wait_ge(acc_added, m - (ES - 1))
                        y = ps[:, 6 + k % SN, :]
                        act.activation(tbuf[:, ES + k % ES, :], y, ACT.Exp, scale=float(K)).then_inc(exp_y_ready, 1)
                    k = i - STATS - 1
                    if 0 <= k < NG and head + 1 < K:
                        source_row(head + 1, k, k % 4)
                    k = i - SHIFT
                    if 0 <= k < NG:
                        act.wait_ge(shift_ready[1 + head], k + 1)
                        for b in range(k * BPG, (k + 1) * BPG):
                            act.activation(Yw[:, b, :], Yw[:, b, :], ACT.Identity, scale=rstd[:, b:b + 1],
                                           bias=shift[:, b:b + 1]).then_inc(att_ready, 1)
                    k = i - ELU - 3
                    if 0 <= k < NG and head == K - 1:
                        act.wait_ge(shift_ready[LAST], k + 1)
                        for b in range(k * BPG, (k + 1) * BPG):
                            last = act.activation(acc[:, b, :], acc[:, b, :], ACT.Identity, scale=r2[:, b:b + 1],
                                                  bias=shift[:, b:b + 1])
                        last.then_inc(out_ready, 1)

            for s in range(SN):
                act.wait_ge(mask_stored[s], 16 * (B // SN) + STORE_CREDIT)
            n = passes(act)
            for head in range(K):
                with act.Fori(n * head, n * (head + 1)) as q:
                    act.wait_ge(below_ready, q + 1)
                    act.activation(ratio[:, :], below[:, :], ACT.Exp, scale=1.0 - SLOPE)
                    act.activation(weight[:, :], below[:, :], ACT.Exp, scale=SLOPE).then_inc(exp_ready, 1)
                    act.wait_ge(exp_ready, q + 1)

                    def exp_row(k):
                        act.wait_ge(rows_clamped, q * NG + (k + 1))
                        act.activation(Rrow[:, cols(k, GW)], Rrow[:, cols(k, GW)], ACT.Exp, scale=1.0 - SLOPE)\
                            .then_inc(R_ready, 1)

                    def relus(g, c):
                        at = q * GC + g * NC + c
                        act.wait_ge(chunk_done, at + 1)
                        if c == 0:
                            act.wait_ge(R_ready, q * NG + (g + 1))
                        act.sem_inc(relus_started, 1)
                        for j in range(JC):
                            last = act.activation(T[:, c % TS, j, :], row_of(Rrow, g), ACT.Relu,
                                                  scale=ratio[:, c * JC + j:c * JC + j + 1], bias=small[:, 8:9])
                        last.then_inc(relu_made, 1)

                    def exp_scale(g):
                        act.wait_ge(row_step, (q * NG + g) * ROW_STEPS + 4)
                        act.activation(scale_row[:, :], above[:, :], ACT.Exp, scale=-1.0).then_inc(scale_row_ready, 1)

                    def sums_to_den(g):
                        act.wait_ge(den_done, q * NG + (g + 1))
                        act.activation(row_of(den, g), bank(g), ACT.Copy).then_inc(den_read, 1)

                    exp_row(0)
                    if head:
                        act.wait_ge(acc_added, head * NG)
                    for c in range(NC):
                        relus(0, c)
                        if c + 1 < NG:
                            exp_row(c + 1)
                    with act.Fori(1, NG) as g:
                        for c in range(NC):
                            relus(g, c)
                            if c == min(1, NC - 1):
                                exp_scale(g - 1)
                            if c == NC - 1:
                                sums_to_den(g - 1)
                    exp_scale(NG - 1)
                    sums_to_den(NG - 1)
                head_end(head)

        @block.vector
        def _(v):
            steps = [0]

            def step(instruction):
                steps[0] += 1
                instruction.then_inc(dve_step, 1)
                v.wait_ge(dve_step, steps[0])

            v.sem_inc(rowsum_done, ROW_CREDIT)
            v.sem_inc(mask_made, MASK_CREDIT)
            v.sem_inc(t_made, TS)
            v.memset(zeros[:, :], 0.0).then_inc(zeros_ready, 1)
            v.memset(small[:, 8:9], -1.0).then_inc(zeros_ready, 1)
            v.wait_ge(ident_ready, 4)
            DS = 5
            with v.Fori(0, NI) as i:
                for u in range(RING):
                    b = i * RING + u
                    v.wait_ge(row_loaded[u % 2], i * 32 + 16 * (u // 2 + 1))
                    v.tensor_reduce(part[:, :], rowbuf[:, u % 2, :].rearrange("p (a n) -> p a n", a=8), AX_X, ALU.add)\
                        .then_inc(rowsum_done, 1)
                    v.wait_ge(rowsum_done, b + (1 + ROW_CREDIT))
                    v.tensor_reduce(small[:, 0:1], part[:, :], AX_X, ALU.add).then_inc(deg_step, 1)
                    v.wait_ge(deg_step, b * DS + 1)
                    v.tensor_scalar(small[:, 1:2], small[:, 0:1], 1.0, TINY, ALU.add, ALU.max).then_inc(deg_ready, 1)
                    v.tensor_scalar(small[:, 2:3], small[:, 0:1], 1.0, 0.0, ALU.add, ALU.is_gt).then_inc(deg_step, 1)
                    v.wait_ge(deg_step, b * DS + 2)
                    v.wait_ge(pow_ready, b + 1)
                    d = d_all[:, bass.ds(b, 1)]
                    v.tensor_tensor(small[:, 4:5], small[:, 3:4], small[:, 2:3], ALU.mult).then_inc(deg_step, 1)
                    v.wait_ge(deg_step, b * DS + 3)
                    v.tensor_copy(d, small[:, 4:5]).then_inc(deg_step, 1)
                    v.tensor_tensor(small[:, 5:6], small[:, 4:5], small[:, 1:2], ALU.mult).then_inc(deg_step, 1)
                    v.wait_ge(deg_step, b * DS + 5)
                    v.wait_ge(pe_block, b + 1)
                    v.wait_ge(xw_ready, i + 1)
                    v.tensor_scalar(stat[:, u, :], block_of(xw_g, b), small[:, 4:5], None, ALU.mult)
                    v.tensor_scalar(diag[:, u, :], ident[:, :], small[:, 5:6], None, ALU.mult).then_inc(stat_ready, 1)
            step(v.tensor_tensor(d2_all[:, :], d_all[:, :], d_all[:, :], ALU.mult))
            v.wait_ge(consts, ALL_CONSTS)
            step(v.tensor_tensor(vec[:, 4:5], vec[:, 1:2], vec[:, 0:1], ALU.subtract))
            step(v.tensor_scalar(vec[:, 4:5], vec[:, 4:5], 1.0 / C, None, ALU.mult))
            v.tensor_scalar(ff1T[:, :, :], ff1T[:, :, :], 1.0 / K, None, ALU.mult)
            v.tensor_scalar(gain_mix[:, :], ident[:, :], vec[:, 0:1], vec[:, 4:5], ALU.mult, ALU.add).then_inc(gain_mix_ready, 1)
            for k in range(NG):
                v.wait_ge(hw_done, k + 1)
                v.tensor_tensor(xw_g[:, group(k), :], ps[:, k, :].rearrange("p (b c) -> p b c", c=C),
                                bcast(d2_all[:, group(k)], C), ALU.mult).then_inc(g_ready, 1)
            v.wait_ge(weights_read, 2)
            for head in range(K):
                v.tensor_copy(was[:, head, :], wa[:, 2 * head:2 * head + 1].broadcast_to([P, P])).then_inc(was_ready, 1)
            def make_mask(turn, block, b, tile, stored):
                v.wait_ge(mask_stored[tile], stored)
                v.tensor_scalar(mtile[:, tile, :], block, 0.0, None, ALU.is_gt).then_inc(tile_step, 1)
                v.wait_ge(tile_step, turn + 1)
                own = mtile[:, tile, bass.ds(b * P, P)]
                v.tensor_tensor(own, own, ident_u8[:, :], ALU.max).then_inc(mask_made, 1)

            for turn, (u, b) in enumerate(FIRST_TURNS):
                if turn >= RING:
                    v.wait_ge(row_loaded[u], NI * 32 + 16)
                make_mask(turn, (rowbuf if turn >= RING else colbuf)[:, u, :], b, turn % SN, 16 * (turn // SN + 1))
            with v.Fori(0, ROUNDS) as i:
                for u in range(RING):
                    v.wait_ge(col_loaded[u], i * 16 + 16 * (NI + 1))
                    make_mask(i * RING + (len(FIRST_TURNS) + u), colbuf[:, u, :], i * RING + (AHEAD + u), u % SN,
                              i * 32 + 16 * ((len(FIRST_TURNS) + u) // SN + 1))
            for u in range(LATE):
                v.wait_ge(col_loaded[u], 16 * (NI + 1 + ROUNDS))
                make_mask(B - LATE + u, colbuf[:, u, :], ROUNDS * RING + AHEAD + u, u % SN, 16 * ((B - LATE + u) // SN + 1))

            def stats(z, k, source):
                v.wait_ge(rows_ready[z], k + 1)
                for b in range(k * BPG, (k + 1) * BPG):
                    last = v.bn_stats(bn[:, z // LAST, b, :], source(b))
                last.then_inc(stats_ready[z], 1)

            def moments(z, k):
                v.wait_ge(stats_ready[z], k + 1)
                for b in range(k * BPG, (k + 1) * BPG):
                    last = v.bn_aggr(mv[:, z // LAST, b, :], bn[:, z // LAST, b, :])
                last.then_inc(moments_ready[z], 1)

            def shifts(z, k, scale):
                v.wait_ge(scale_ready[z], k + 1)
                v.scalar_tensor_tensor(out=shift[:, group(k)], in0=mv[:, z // LAST, group(k), 0], scalar=-1.0,
                                       in1=scale[:, group(k)], op0=ALU.mult, op1=ALU.mult)\
                    .then_inc(shift_ready[z], 1)

            v.wait_ge(skip_ready, 3)
            for i in range(NG + 3):
                k = i
                if k < NG:
                    v.wait_ge(tr_done, k + 1)
                    for b in range(k * BPG, (k + 1) * BPG):
                        last = v.scalar_tensor_tensor(out=x1[:, b, :], in0=ps[:, k, cols(b % BPG)],
                                                      scalar=d_all[:, b:b + 1], in1=x1[:, b, :],
                                                      op0=ALU.mult, op1=ALU.add)
                    last.then_inc(rows_ready[0], 1)
                if 0 <= i - STATS < NG:
                    stats(0, i - STATS, lambda b: x1[:, b, :])
                if 0 <= i - MOMENTS < NG:
                    moments(0, i - MOMENTS)
                if 0 <= i - SHIFT < NG:
                    k = i - SHIFT
                    v.wait_ge(scale_ready[0], k + 1)
                    for b in range(k * BPG, (k + 1) * BPG):
                        last = v.tensor_scalar(x1[:, b, :], x1[:, b, :], mv[:, 0, b, 0:1], rstd[:, b:b + 1],
                                               ALU.subtract, ALU.mult)
                    last.then_inc(x1_ready, 1)

            v.wait_ge(st_ready, NG)
            for head in range(K):
                v.tensor_reduce(span[:, head:head + 1], st[:, :, 2 * head + 1], AX_X, ALU.max)
                last = v.tensor_reduce(span[:, K + head:K + head + 1], st[:, :, 2 * head + 1], AX_X, ALU.min)
            step(last)
            v.tensor_scalar(span[:, K:2 * K], span[:, K:2 * K], -1.0, None, ALU.mult).then_inc(span_ready, 1)
            v.wait_ge(top_ready, 1)
            step(v.tensor_tensor(npass_f[:, :], top[:, 0:K], top[:, K:2 * K], ALU.add))
            step(v.tensor_reduce(small[:, 6:7], npass_f[:, :], AX_X, ALU.max))
            step(v.tensor_scalar(small[:, 7:8], small[:, 6:7], 1.0 / WINDOW, 1.1, ALU.mult, ALU.add))
            v.tensor_copy(npass[:, :], small[:, 7:8]).then_inc(npass_ready, 1)

            def head_end(head):
                z = 1 + head
                v.wait_ge(den_step, n * (3 * (head + 1) * NG))
                for i in range(NG + END):
                    k = i
                    if k < NG:
                        v.wait_ge(att_h_done, head * NG + k + 1)
                        for b in range(k * BPG, (k + 1) * BPG):
                            last = v.scalar_tensor_tensor(out=Yw[:, b, :], in0=ps[:, k % 4, cols(b % BPG)],
                                                          scalar=inv_den[:, b:b + 1], in1=x1[:, b, :],
                                                          op0=ALU.mult, op1=ALU.add)
                        last.then_inc(rows_ready[z], 1)
                    if 0 <= i - STATS < NG:
                        stats(z, i - STATS, lambda b: Yw[:, b, :])
                    if 0 <= i - MOMENTS < NG:
                        moments(z, i - MOMENTS)
                    k = i - SHIFT
                    if 0 <= k < NG:
                        shifts(z, k, rstd)
                    k = i - ELU
                    if 0 <= k < NG:
                        e = tbuf[:, ES + k % ES, :]
                        v.wait_ge(exp_y_ready, head * NG + k + 1)
                        step(v.tensor_scalar(e, e, 1.0, 1.0 / K, ALU.min, ALU.mult))
                        v.scalar_tensor_tensor(out=e, in0=e, scalar=-1.0 / K, in1=ps[:, 6 + k % SN, :],
                                               op0=ALU.add, op1=ALU.max).then_inc(elu_ready, 1)
                    if head == K - 1:
                        k = i - ELU - 1
                        if 0 <= k < NG:
                            v.wait_ge(acc_added, head * NG + k + 1)
                            for b in range(k * BPG, (k + 1) * BPG):
                                last = v.bn_stats(bn[:, 1, b, :], acc[:, b, :])
                            last.then_inc(stats_ready[LAST], 1)
                        if 0 <= k - 1 < NG:
                            moments(LAST, k - 1)
                        if 0 <= k - 2 < NG:
                            shifts(LAST, k - 2, r2)

            n = passes(v)
            v.wait_ge(srow_ready, NG)
            for head in range(K):
                step(v.tensor_copy(gref[:, 0:1], top[:, head:head + 1]))
                if head:
                    v.wait_ge(srow_ready, K * NG)
                    v.wait_ge(att_t_done, head * NG)
                with v.Fori(n * head, n * (head + 1)) as q:
                    done = [0]

                    def pstep(instruction):
                        done[0] += 1
                        instruction.then_inc(pass_step, 1)
                        v.wait_ge(pass_step, q * PASS_STEPS + done[0])

                    v.wait_ge(relu_made, q * GC + 1)
                    v.wait_ge(chunk_done, q * GC + TS)
                    v.wait_ge(den_read, q * NG + NG)
                    s_dst = st[:, :, 2 * head + 1]
                    pstep(v.tensor_scalar(gref[:, 1:2], gref[:, 0:1], -WINDOW, None, ALU.add))
                    v.tensor_scalar(below[:, :], s_dst, gref[:, 0:1], 0.0, ALU.subtract, ALU.min).then_inc(below_ready, 1)
                    pstep(v.tensor_scalar(inside[:, :], s_dst, gref[:, 0:1], None, ALU.is_le))
                    pstep(v.scalar_tensor_tensor(out=inside[:, :], in0=s_dst, scalar=gref[:, 1:2], in1=inside[:, :],
                                                 op0=ALU.is_gt, op1=ALU.mult))

                    def clamp_row(k):
                        v.tensor_scalar(Rrow[:, cols(k, GW)], srow[:, head, cols(k, GW)], gref[:, 0:1], WINDOW,
                                        ALU.add, ALU.min).then_inc(rows_clamped, 1)

                    def weigh(c):
                        for b in range(c * JC, (c + 1) * JC):
                            last = v.tensor_scalar(Yw[:, b, :], x1[:, b, :], r2w[:, b:b + 1], weight[:, b:b + 1],
                                                   ALU.mult, ALU.add)
                        last.then_inc(yw_ready, 1)

                    def chunk(g, c):
                        at = q * GC + g * NC + c
                        v.wait_ge(mask_loaded[c % TS], (q * NG + g) * (16 * USES[c % TS]) + 16 * (c // TS + 1))
                        v.wait_ge(relu_made, at + 2)
                        tile = T[:, c % TS, :, :].rearrange("p b n -> p (b n)")
                        v.scalar_tensor_tensor(out=tile, in0=tile, scalar=1.0,
                                               in1=mring[:, c % TS, :, :].rearrange("p b n -> p (b n)"),
                                               op0=ALU.add, op1=ALU.mult).then_inc(t_made, 1)

                    def row_scale(g, stage):
                        at = (q * NG + g) * ROW_STEPS
                        s_src, own_ref = srow[:, head, bass.ds(g * GW, GW)], row_of(ref, g)
                        if stage == 0:
                            v.tensor_scalar(log_scale[:, :], s_src, gref[:, 0:1], None, ALU.add)
                            v.tensor_scalar(above[:, :], s_src, gref[:, 0:1], WINDOW, ALU.add, ALU.min)\
                                .then_inc(row_step, 1)
                        elif stage == 1:
                            v.wait_ge(row_step, at + 1)
                            v.scalar_tensor_tensor(out=log_scale[:, :], in0=above[:, :], scalar=SLOPE - 1.0,
                                                   in1=log_scale[:, :], op0=ALU.mult, op1=ALU.add).then_inc(row_step, 1)
                        elif stage == 2:
                            v.wait_ge(sums_zeroed, 2 * head + 3)
                            v.wait_ge(row_step, at + 2)
                            v.tensor_tensor(above[:, :], own_ref, log_scale[:, :], ALU.subtract).then_inc(row_step, 1)
                        else:
                            v.wait_ge(row_step, at + 3)
                            v.scalar_tensor_tensor(out=above[:, :], in0=row_of(den, g), scalar=0.0, in1=above[:, :],
                                                   op0=ALU.is_gt, op1=ALU.mult).then_inc(row_step, 1)
                            v.wait_ge(row_step, at + 4)
                            v.tensor_tensor(own_ref, log_scale[:, :], above[:, :], ALU.add).then_inc(row_step, 1)

                    def add_sums(g):
                        v.wait_ge(chunk_done, (q * NG + g) * NC + (NC + TS))
                        v.wait_ge(scale_row_ready, q * NG + (g + 1))
                        v.tensor_tensor(scaled[:, :], bank(g), scale_row[:, :], ALU.mult).then_inc(sum_step, 1)
                        v.wait_ge(sum_step, q * NG + (g + 1))
                        v.tensor_tensor(row_of(num, g), row_of(num, g), scaled[:, :], ALU.add).then_inc(num_ready, 1)

                    def invert_den(g):
                        at = (q * NG + g) * 3
                        v.wait_ge(den_read, q * NG + (g + (1 + NG)))
                        v.tensor_tensor(scaled[:, :].rearrange("p (b n) -> p b n", n=P),
                                        row_of(den, g).rearrange("p (b n) -> p b n", n=P),
                                        ident[:, :].unsqueeze(1).broadcast_to([P, BPG, P]), ALU.mult).then_inc(den_step, 1)
                        v.wait_ge(den_step, at + 1)
                        v.tensor_reduce(node_den[:, :], scaled[:, :].rearrange("p (b n) -> p b n", n=P), AX_X, ALU.add)\
                            .then_inc(den_step, 1)
                        v.wait_ge(den_step, at + 2)
                        v.reciprocal(inv_den[:, bass.ds(g * BPG, BPG)], node_den[:, :]).then_inc(den_step, 1)

                    clamp_row(0)
                    v.wait_ge(exp_ready, q + 1)
                    pstep(v.tensor_tensor(weight[:, :], weight[:, :], inside[:, :], ALU.mult))
                    pstep(v.tensor_tensor(r2w[:, :], weight[:, :], r2[:, :], ALU.mult))
                    assert done[0] == PASS_STEPS
                    weigh(0)
                    for c in range(NC):
                        if c + 1 < NC:
                            clamp_row(c + 1)
                        chunk(0, c)
                        if c + 1 < NC:
                            weigh(c + 1)
                        for stage in range(4):
                            if c == max(NC - 4 + stage, 0):
                                row_scale(0, stage)
                    with v.Fori(1, NG) as g:
                        for c in range(NC):
                            chunk(g, c)
                            if c == NC // 2 - 1:
                                add_sums(g - 1)
                            if c == NC - 1:
                                invert_den(g - 1)
                            for stage in range(4):
                                if c == max(NC - 4 + stage, 0):
                                    row_scale(g, stage)
                    add_sums(NG - 1)
                    v.tensor_copy(gref[:, 0:1], gref[:, 1:2]).then_inc(gref_moved, 1)
                    invert_den(NG - 1)
                    v.wait_ge(gref_moved, q + 1)
                head_end(head)

        @block.tensor
        def _(pe):
            def multiply(*args, **kw):
                return pe.matmul(*args, skip_group_check=True, **kw)

            def zero_banks(start, stop, k):
                return multiply(ps[:, k, :], zeros[:, 0:P], zeros[:, :], start=start, stop=stop)

            def aggregate(u, blocks):
                for k in range(NG):
                    last = multiply(ps[:, k, :], stat[:, u, :], blocks[:, u, cols(k, GW)], start=False, stop=False)
                return last

            def add_own(own, u):
                multiply(own, stat[:, u, :], ident[:, :], start=False, stop=False)
                return multiply(own, b1bc[:, :], diag[:, u, :], start=False, stop=False)

            def times_w2(k):
                pe.wait_ge(hT_ready, k + 1)
                for ib in range(BPG):
                    last = multiply(ps[:, k, cols(ib)], hT[:, k % SN, cols(ib)], w2[:, :], start=True, stop=True)
                last.then_inc(hw_done, 1)

            def spread_source(head, k, at):
                if k == 0:
                    pe.wait_ge(was_ready, head + 1)
                multiply(ps[:, at, :], was[:, head, :], xnT[:, cols(k, GW)], start=True, stop=True).then_inc(s_done, 1)

            pe.sem_inc(pe_block, COL_CREDIT)
            pe.sem_inc(chunk_done, TS)
            pe.wait_ge(first_loaded, ALL_FIRST)
            pe.wait_ge(ident_ready, 4)
            for i in range(NG + 1):
                k = i
                if k < NG:
                    pe.wait_ge(x_loaded[k], 16)
                    for b in range(k * BPG, (k + 1) * BPG):
                        last = pe.transpose(ps[:, k, cols(b % BPG)], x1[:, b, :], ident[:, :])
                    last.then_inc(xT_done, 1)
                k = i - 1
                if k >= 0:
                    pe.wait_ge(xT_ready, k + 1)
                    for b in range(k * BPG, (k + 1) * BPG):
                        last = multiply(ps[:, k, cols(b % BPG)], xnT[:, cols(b)], w1[:, :], start=True, stop=True)
                    last.then_inc(xw_done, 1)
            pe.wait_ge(zeros_ready, 2)
            for k in range(NG):
                pe.wait_ge(xw_ready, k + 1)
                zero_banks(True, False, k)
            with pe.Fori(0, NI - 1) as i:
                for u in range(RING):
                    pe.wait_ge(col_loaded[u], i * 16 + 16)
                    pe.wait_ge(stat_ready, i * RING + (u + 1))
                    aggregate(u, colbuf)
                    add_own(ps[:, bass.ds(i, 1), cols(u)].rearrange("p o n -> p (o n)"), u).then_inc(pe_block, 1)
            for u in range(RING):
                pe.wait_ge(col_loaded[u], NI * 16)
                pe.wait_ge(stat_ready, (NI - 1) * RING + (u + 1))
                if u < RING - 1:
                    aggregate(u, colbuf)
                    add_own(ps[:, NG - 1, cols(u)], u).then_inc(pe_block, 1)
            add_own(ps[:, NG - 1, cols(u)], u)
            pe.wait_ge(consts, ALL_CONSTS)
            for i in range(NG + SN):
                k = i
                if k < NG:
                    last = multiply(ps[:, k, :], stat[:, u, :], colbuf[:, u, cols(k, GW)], start=False, stop=k < NG - 1)
                    last.then_inc(agg_done if k < NG - 1 else pe_block, 1)
                if k == NG - 1:
                    multiply(ps[:, k, 0:2], zeros[:, 0:P], zeros[:, 0:2], start=False, stop=True).then_inc(agg_done, 1)
                if 0 <= i - SN < NG:
                    times_w2(i - SN)
            pe.wait_ge(g_ready, 1)
            pe.wait_ge(gain_mix_ready, 1)
            for head in range(K):
                multiply(ps[:, 0, cols(head)], gain_mix[:, :], ff0T[:, head, :], start=True, stop=True)
            for head in range(K):
                last = multiply(ps[:, 0, K * C + 2 * head:K * C + 2 * head + 2], ff0[:, head, :], attnT[:, head, :],
                                start=True, stop=True)
            last.then_inc(weights_done, 1)
            for k in list(range(1, NG)) + [0]:
                pe.wait_ge(g_ready, k + 1)
                if k == 0:
                    pe.wait_ge(weights_read, 2)
                zero_banks(True, False, k)
            for turn, (u, b) in enumerate(FIRST_TURNS):
                pe.wait_ge(g_copied, turn + 1)
                if turn >= RING:
                    pe.wait_ge(row_loaded[u], NI * 32 + 16)
                aggregate(u, rowbuf if turn >= RING else colbuf).then_inc(pe_block, 1)
            with pe.Fori(0, ROUNDS) as i:
                for u in range(RING):
                    pe.wait_ge(col_loaded[u], i * 16 + 16 * (NI + 1))
                    pe.wait_ge(g_copied, i * RING + (len(FIRST_TURNS) + u + 1))
                    aggregate(u, colbuf).then_inc(pe_block, 1)
            for u in range(LATE):
                pe.wait_ge(col_loaded[u], 16 * (NI + 1 + ROUNDS))
                pe.wait_ge(g_copied, B - LATE + u + 1)
            for i in range(NG + TURN + 4):
                k = i
                if k < NG:
                    for u in range(LATE):
                        last = multiply(ps[:, k, :], stat[:, u, :], colbuf[:, u, cols(k, GW)],
                                        start=False, stop=u == LATE - 1)
                    last.then_inc(agg_done, 1)
                k = i - 1
                if 0 <= k < NG:
                    pe.wait_ge(accT_ready, k + 1)
                    for ib in range(BPG):
                        last = pe.transpose(ps[:, k, cols(ib)], hT[:, k % SN, cols(ib)], ident[:, :])
                    last.then_inc(tr_done, 1)
                k = i - TURN - 1
                if 0 <= k < NG:
                    pe.wait_ge(xn_ready, (k + 1) * BPG)
                    for ib in range(BPG):
                        last = pe.transpose(ps[:, k, cols(ib)], Yw[:, k * BPG + ib, :], ident[:, :])
                    last.then_inc(xnt_done, 1)
                k = i - TURN - 2
                if 0 <= k < NG:
                    pe.wait_ge(xnT_ready, k + 1)
                    for ib in range(BPG):
                        last = multiply(ps[:, k, cols(ib, 2 * K)], xnT[:, cols(k * BPG + ib)], wa[:, :],
                                        start=True, stop=True)
                    last.then_inc(st_done, 1)
                k = i - TURN - 3
                if 0 <= k < NG:
                    pe.wait_ge(st_ready, k + 1)
                    spread_source(0, k, k)
            pe.wait_ge(srow_ready, NG)
            pe.wait_ge(mean_ready, 1)
            n = passes(pe)
            for head in range(K):
                with pe.Fori(n * head, n * (head + 1)) as q:
                    def chunk(g, c):
                        at = q * GC + g * NC + c
                        pe.wait_ge(t_made, at + (TS + 1))
                        if c == 0:
                            pe.wait_ge(den_read, q * NG + (g + 1))
                        for j in range(JC):
                            last = multiply(bank(g), Yw[:, c * JC + j, :], T[:, c % TS, j, :],
                                            start=c == 0 and j == 0, stop=c == NC - 1 and j == JC - 1)
                        last.then_inc(chunk_done, 1)

                    def spread_den(g):
                        pe.wait_ge(num_ready, q * NG + (g + 1))
                        multiply(bank(g), mean[:, :], row_of(num, g), start=True, stop=True).then_inc(den_done, 1)

                    for c in range(NC):
                        pe.wait_ge(yw_ready, q * NC + (c + 1))
                        chunk(0, c)
                    with pe.Fori(1, NG) as g:
                        for c in range(NC):
                            chunk(g, c)
                            if c == NC // 2 - 1:
                                spread_den(g - 1)
                    spread_den(NG - 1)
                for i in range(NG + SHIFT + 2):
                    k = i
                    if k < NG:
                        if k == 0:
                            pe.wait_ge(den_read, n * ((head + 1) * NG) + (NG - 1))
                        if k == min(4, NG - 1):
                            pe.wait_ge(den_read, n * ((head + 1) * NG) + NG)
                        if k >= 4:
                            pe.wait_ge(rows_ready[1 + head], k - 3)
                            if head + 1 < K:
                                pe.wait_ge(srow_ready, (head + 1) * NG + k - 3)
                        for ib in range(BPG):
                            last = multiply(ps[:, k % 4, cols(ib)], num[:, cols(k * BPG + ib)], fold[:, head, :],
                                            start=True, stop=True)
                        last.then_inc(att_h_done, 1)
                    k = i - STATS - 1
                    if 0 <= k < NG and head + 1 < K:
                        pe.wait_ge(rows_ready[1 + head], k + 1)
                        spread_source(head + 1, k, k % 4)
                    k = i - SHIFT - 1
                    if 0 <= k < NG:
                        m = head * NG + k
                        pe.wait_ge(att_ready, (m + 1) * BPG)
                        if k >= SN:
                            pe.wait_ge(att_t_ready, m - 1)
                        for ib in range(BPG):
                            last = pe.transpose(ps[:, 4 + k % SN, cols(ib)], Yw[:, k * BPG + ib, :], ident[:, :])
                        last.then_inc(att_t_done, 1)
                    k = i - SHIFT - 2
                    if 0 <= k < NG:
                        m = head * NG + k
                        pe.wait_ge(att_t_ready, m + 1)
                        if k >= SN:
                            pe.wait_ge(elu_ready, m - 1)
                        for ib in range(BPG):
                            last = multiply(ps[:, 6 + k % SN, cols(ib)], tbuf[:, k % ES, cols(ib)],
                                            ff1T[:, head, :], start=True, stop=True)
                        last.then_inc(y_done, 1)
                if head + 1 < K:
                    pe.wait_ge(srow_ready, (head + 2) * NG)
                    pe.wait_ge(elu_ready, (head + 1) * NG)


_INS = ["x", "adj", "adjT", "W1", "b1", "W2", "b2", "ff0", "ff0T", "ff1T", "attnT",
        "ln1_g", "ln1_b", "ln2_g", "ln2_b"]


def kernel(x, adj, L0_gnn_W1, L0_gnn_b1, L0_gnn_W2, L0_gnn_b2, L1_gnn_ff0_w, L1_gnn_ff1_w, L1_gnn_attn_w,
           L1_gnn_g1, L1_gnn_b1, L1_gnn_g2, L1_gnn_b2):
    import numpy as np
    from concourse import bacc
    from concourse.bass_utils import run_bass_kernel_spmd

    ff0, ff1, attn = np.asarray(L1_gnn_ff0_w), np.asarray(L1_gnn_ff1_w), np.asarray(L1_gnn_attn_w)
    heads, c = ff0.shape[0], ff0.shape[1]
    given = {
        "x": x, "adj": adj, "adjT": np.asarray(adj).T,
        "W1": L0_gnn_W1, "b1": L0_gnn_b1, "W2": L0_gnn_W2, "b2": L0_gnn_b2,
        "ff0": ff0, "ff0T": ff0.transpose(0, 2, 1), "ff1T": ff1.transpose(0, 2, 1),
        "attnT": attn.reshape(heads, 2, c).transpose(2, 0, 1),
        "ln1_g": L1_gnn_g1, "ln1_b": L1_gnn_b1, "ln2_g": L1_gnn_g2, "ln2_b": L1_gnn_b2,
    }
    arrays = {name: np.ascontiguousarray(given[name]) for name in _INS}
    nc = bacc.Bacc("TRN2", target_bir_lowering=False, num_devices=1)
    t = {name: nc.dram_tensor(f"in_{name}", arrays[name].shape, F32, kind="ExternalInput").ap() for name in _INS}
    out = nc.dram_tensor("out", arrays["x"].shape, F32, kind="ExternalOutput").ap()
    build(nc, t, out)
    r = run_bass_kernel_spmd(nc, [{f"in_{name}": a for name, a in arrays.items()}], core_ids=[0])
    return r.results[0]["out"]
```
